# Optimizing a Trainium2 kernel written in Bass

```python
import numpy as np
import jax
import jax.numpy as jnp

def _softmax(x, axis=-1):
    return jax.nn.softmax(x, axis=axis)

def _gelu(x):
    return jax.nn.gelu(x, approximate=True)

def _silu(x):
    return jax.nn.silu(x)

def _sigmoid(x):
    return jax.nn.sigmoid(x)

def _layernorm(x, axis=-1, eps=1e-05):
    m = jnp.mean(x, axis=axis, keepdims=True)
    v = jnp.var(x, axis=axis, keepdims=True)
    return (x - m) / jnp.sqrt(v + eps)

def _scatter_add(tgt, idx, src, axis=0):
    return tgt.at[idx].add(src)

def _segment_sum(src, seg, n):
    return jax.ops.segment_sum(src, seg, n)
kernel_name = 'mk_decoder_preln_d1_seqx_r4_16bc66'

def setup_inputs(seed: int=0):
    np.random.seed(seed)
    _w = jnp.asarray

    def _rec_inputs():
        import jax
        import jax.numpy as jnp
        _rk = jax.random.key(seed)
        x = -0.0003929 + 0.9999 * jax.random.normal(jax.random.fold_in(_rk, 1), (8, 256, 1024), jnp.float32)
        _lenS = 256 - jax.random.randint(jax.random.fold_in(_rk, 7), (8,), 0, max(1, 256 // 4) + 1, jnp.int32)
        _lenS2 = 256 - jax.random.randint(jax.random.fold_in(_rk, 8), (8,), 0, max(1, 256 // 4) + 1, jnp.int32)
        _ctx_4096P = jax.random.normal(jax.random.fold_in(_rk, 11), (8, 16, 1024), jnp.float32)
        _ctx_4096c = jax.random.dirichlet(jax.random.fold_in(_rk, 511), 0.3 * jnp.ones((16,), jnp.float32), (8, 256))
        _ctx_4096t = jnp.einsum('bsk,bkd->bsd', _ctx_4096c, _ctx_4096P)
        _ctx_4096t = _ctx_4096t * jax.lax.rsqrt(jnp.mean(jnp.square(_ctx_4096t)) + 1e-12) * 0.953939
        ctx_4096 = 2.81802e-05 + 1.00001 * (_ctx_4096t + 0.3 * jax.random.normal(jax.random.fold_in(_rk, 611), (8, 256, 1024), jnp.float32))
        return (x, ctx_4096)
    x, ctx_4096 = _rec_inputs()

    def _L0_attn_setup():
        import jax, jax.numpy as jnp
        import numpy as np
        HIDDEN = 1024
        NHQ = 32
        NHKV = 8
        HEAD_DIM = HIDDEN // NHQ
        THETA = 10000.0

        def _rope(x, theta_base):
            b, h, s, d = x.shape
            inv_freq = 1.0 / theta_base ** (jnp.arange(0, d, 2, dtype=jnp.float32)[:d // 2] / d)
            freqs = jnp.arange(s, dtype=jnp.float32)[:, None] * inv_freq[None, :]
            cos = jnp.cos(freqs).astype(x.dtype)
            sin = jnp.sin(freqs).astype(x.dtype)
            x1, x2 = (x[..., :d // 2], x[..., d // 2:])
            return jnp.concatenate([x1 * cos - x2 * sin, x2 * cos + x1 * sin], axis=-1)
        key = jax.random.key(seed)
        ks = jax.random.split(key, 5)
        std = 1.0 / np.sqrt(HIDDEN)
        x = jax.random.normal(ks[0], (2, 512, HIDDEN), dtype=jnp.float32)
        Wq = jax.random.normal(ks[1], (HIDDEN, HIDDEN), dtype=jnp.float32) * std
        Wk = jax.random.normal(ks[2], (HIDDEN, NHKV * HEAD_DIM), dtype=jnp.float32) * std
        Wv = jax.random.normal(ks[3], (HIDDEN, NHKV * HEAD_DIM), dtype=jnp.float32) * std
        Wo = jax.random.normal(ks[4], (HIDDEN, HIDDEN), dtype=jnp.float32) * std
        return {'x': x, 'Wq': Wq, 'Wk': Wk, 'Wv': Wv, 'Wo': Wo}
    _L0_attn_all = _L0_attn_setup()
    _L0_attn_in = {k: v for k, v in _L0_attn_all.items() if k in ('Wq', 'Wk', 'Wv', 'Wo')}
    del _L0_attn_all

    def _L0_xattn_setup():
        import jax, jax.numpy as jnp
        import numpy as np
        EMBED = 1024
        NUM_Q = 32
        NUM_KV = 8
        GROUPS = NUM_Q // NUM_KV
        HEAD_DIM = EMBED // NUM_Q
        KV_DIM = HEAD_DIM * NUM_KV
        key = jax.random.key(seed)
        ks = jax.random.split(key, 12)
        B, S = (2, 512)
        s = 0.02
        return {'query': jax.random.normal(ks[0], (B, S, EMBED), jnp.float32), 'key': jax.random.normal(ks[1], (B, S, EMBED), jnp.float32), 'value': jax.random.normal(ks[2], (B, S, EMBED), jnp.float32), 'Wq': jax.random.normal(ks[3], (EMBED, EMBED), jnp.float32) * s, 'bq': jnp.zeros((EMBED,), jnp.float32), 'Wk': jax.random.normal(ks[4], (EMBED, KV_DIM), jnp.float32) * s, 'bk': jnp.zeros((KV_DIM,), jnp.float32), 'Wv': jax.random.normal(ks[5], (EMBED, KV_DIM), jnp.float32) * s, 'bv': jnp.zeros((KV_DIM,), jnp.float32), 'Wo': jax.random.normal(ks[6], (EMBED, EMBED), jnp.float32) * s, 'bo': jnp.zeros((EMBED,), jnp.float32)}
    _L0_xattn_all = _L0_xattn_setup()
    _L0_xattn_in = {k: v for k, v in _L0_xattn_all.items() if k in ('Wq', 'bq', 'Wk', 'bk', 'Wv', 'bv', 'Wo', 'bo')}
    del _L0_xattn_all

    def _L0_ffn_setup():
        import jax, jax.numpy as jnp
        import numpy as np
        BLOCK = 128
        FP8_MAX = 448.0

        def _quant_weight(w):
            N, K = w.shape
            wb = w.reshape(N // BLOCK, BLOCK, K // BLOCK, BLOCK)
            ws = jnp.max(jnp.abs(wb), axis=(1, 3)) / FP8_MAX
            ws_full = jnp.repeat(jnp.repeat(ws, BLOCK, axis=0), BLOCK, axis=1)
            w_fp8 = (w / ws_full).astype(jnp.float8_e4m3fn).astype(jnp.float32)
            return (w_fp8, ws)
        key = jax.random.key(seed)
        k1, k2 = jax.random.split(key)
        x = jax.random.normal(k1, (4, 512, 1024), dtype=jnp.float32)
        w = jax.random.normal(k2, (1024, 1024), dtype=jnp.float32) * 0.02
        weight, weight_scale = _quant_weight(w)
        return {'x': x, 'weight': weight, 'weight_scale': weight_scale}
    _L0_ffn_all = _L0_ffn_setup()
    _L0_ffn_in = {k: v for k, v in _L0_ffn_all.items() if k in ('weight', 'weight_scale')}
    del _L0_ffn_all
    return {'x': x, 'ctx_4096': ctx_4096, 'L0_attn_Wq': _L0_attn_in['Wq'], 'L0_attn_Wk': _L0_attn_in['Wk'], 'L0_attn_Wv': _L0_attn_in['Wv'], 'L0_attn_Wo': _L0_attn_in['Wo'], 'L0_xattn_Wq': _L0_xattn_in['Wq'], 'L0_xattn_bq': _L0_xattn_in['bq'], 'L0_xattn_Wk': _L0_xattn_in['Wk'], 'L0_xattn_bk': _L0_xattn_in['bk'], 'L0_xattn_Wv': _L0_xattn_in['Wv'], 'L0_xattn_bv': _L0_xattn_in['bv'], 'L0_xattn_Wo': _L0_xattn_in['Wo'], 'L0_xattn_bo': _L0_xattn_in['bo'], 'L0_ffn_weight': _L0_ffn_in['weight'], 'L0_ffn_weight_scale': _L0_ffn_in['weight_scale']}

def reference(x, ctx_4096, L0_attn_Wq, L0_attn_Wk, L0_attn_Wv, L0_attn_Wo, L0_xattn_Wq, L0_xattn_bq, L0_xattn_Wk, L0_xattn_bk, L0_xattn_Wv, L0_xattn_bv, L0_xattn_Wo, L0_xattn_bo, L0_ffn_weight, L0_ffn_weight_scale):
    import jax
    import jax.numpy as jnp

    def _L0_attn_ref(x, Wq, Wk, Wv, Wo):
        import jax, jax.numpy as jnp
        import numpy as np
        HIDDEN = 1024
        NHQ = 32
        NHKV = 8
        HEAD_DIM = HIDDEN // NHQ
        THETA = 10000.0

        def _rope(x, theta_base):
            b, h, s, d = x.shape
            inv_freq = 1.0 / theta_base ** (jnp.arange(0, d, 2, dtype=jnp.float32)[:d // 2] / d)
            freqs = jnp.arange(s, dtype=jnp.float32)[:, None] * inv_freq[None, :]
            cos = jnp.cos(freqs).astype(x.dtype)
            sin = jnp.sin(freqs).astype(x.dtype)
            x1, x2 = (x[..., :d // 2], x[..., d // 2:])
            return jnp.concatenate([x1 * cos - x2 * sin, x2 * cos + x1 * sin], axis=-1)
        b, s, _ = x.shape
        q_per_kv = NHQ // NHKV
        q = (x @ Wq).reshape(b, s, NHQ, HEAD_DIM).transpose(0, 2, 1, 3)
        k = (x @ Wk).reshape(b, s, NHKV, HEAD_DIM).transpose(0, 2, 1, 3)
        v = (x @ Wv).reshape(b, s, NHKV, HEAD_DIM).transpose(0, 2, 1, 3)
        q = _rope(q, THETA)
        k = _rope(k, THETA)
        qg = q.reshape(b, NHKV, q_per_kv, s, HEAD_DIM)
        scores = jnp.einsum('bkgqd,bkmd->bkgqm', qg, k) / np.sqrt(HEAD_DIM)
        causal = jnp.tril(jnp.ones((s, s), dtype=bool))
        scores = jnp.where(causal, scores, -jnp.inf)
        attn = jax.nn.softmax(scores, axis=-1)
        out = jnp.einsum('bkgqm,bkmd->bkgqd', attn, v)
        out = out.reshape(b, NHQ, s, HEAD_DIM).transpose(0, 2, 1, 3).reshape(b, s, HIDDEN)
        return out @ Wo

    def _L0_xattn_ref(query, key, value, Wq, bq, Wk, bk, Wv, bv, Wo, bo):
        import jax, jax.numpy as jnp
        import numpy as np
        EMBED = 1024
        NUM_Q = 32
        NUM_KV = 8
        GROUPS = NUM_Q // NUM_KV
        HEAD_DIM = EMBED // NUM_Q
        KV_DIM = HEAD_DIM * NUM_KV
        B, S, _ = query.shape
        Q = query @ Wq + bq
        K = key @ Wk + bk
        V = value @ Wv + bv
        Q = Q.reshape(B, S, NUM_KV, GROUPS, HEAD_DIM).transpose(0, 2, 3, 1, 4)
        K = K.reshape(B, S, NUM_KV, HEAD_DIM).transpose(0, 2, 1, 3)
        V = V.reshape(B, S, NUM_KV, HEAD_DIM).transpose(0, 2, 1, 3)
        scale = 1.0 / jnp.sqrt(jnp.asarray(HEAD_DIM, query.dtype))
        scores = jnp.einsum('bhgqd,bhkd->bhgqk', Q, K) * scale
        w = jax.nn.softmax(scores, axis=-1)
        y = jnp.einsum('bhgqk,bhkd->bhgqd', w, V)
        y = y.transpose(0, 3, 1, 2, 4).reshape(B, S, EMBED)
        return y @ Wo + bo

    def _L0_ffn_ref(x, weight, weight_scale):
        import jax, jax.numpy as jnp
        import numpy as np
        BLOCK = 128
        FP8_MAX = 448.0

        def _quant_weight(w):
            N, K = w.shape
            wb = w.reshape(N // BLOCK, BLOCK, K // BLOCK, BLOCK)
            ws = jnp.max(jnp.abs(wb), axis=(1, 3)) / FP8_MAX
            ws_full = jnp.repeat(jnp.repeat(ws, BLOCK, axis=0), BLOCK, axis=1)
            w_fp8 = (w / ws_full).astype(jnp.float8_e4m3fn).astype(jnp.float32)
            return (w_fp8, ws)
        'FP8Linear forward: dynamic per-128-block activation quant + scaled fp8 GEMM.\n\n            x:            [..., K] float32\n            weight:       [N, K]   fp8 values stored as float32\n            weight_scale: [N/128, K/128] float32 per-block weight scales\n            '
        *lead, K = x.shape
        N = weight.shape[0]
        xb = x.reshape(-1, K // BLOCK, BLOCK)
        s = jnp.max(jnp.abs(xb), axis=-1, keepdims=True) / FP8_MAX
        xq = (xb / s).astype(jnp.float8_e4m3fn).astype(jnp.float32)
        a = (xq * s).reshape(-1, K)
        ws_full = jnp.repeat(jnp.repeat(weight_scale, BLOCK, axis=0), BLOCK, axis=1)
        w_deq = weight * ws_full
        y = a @ w_deq.T
        return y.reshape(*lead, N)
    x = x + _L0_attn_ref(_layernorm(x, axis=-1), L0_attn_Wq, L0_attn_Wk, L0_attn_Wv, L0_attn_Wo)
    x = x + _L0_xattn_ref(_layernorm(x, axis=-1), ctx_4096, ctx_4096, L0_xattn_Wq, L0_xattn_bq, L0_xattn_Wk, L0_xattn_bk, L0_xattn_Wv, L0_xattn_bv, L0_xattn_Wo, L0_xattn_bo)
    x = x + _L0_ffn_ref(_layernorm(x, axis=-1), L0_ffn_weight, L0_ffn_weight_scale)
    return x

_drawn_inputs = setup_inputs


def setup_inputs(seed=0):
    import zlib

    import numpy as np

    out = dict(_drawn_inputs(seed))
    spreads = {'L0_xattn_bq': (0.0, 0.8),
     'L0_xattn_bk': (0.0, 0.8),
     'L0_xattn_bv': (0.0, 0.1),
     'L0_xattn_bo': (0.0, 0.1)}
    factors = {}
    for name, (base, spread) in spreads.items():
        noise = np.random.default_rng([zlib.crc32(name.encode()), seed]).standard_normal(out[name].shape)
        drawn = base * np.exp(spread * noise) if base else spread * noise
        out[name] = jnp.asarray(drawn.astype(out[name].dtype))
    for name, factor in factors.items():
        out[name] = (out[name] * factor).astype(out[name].dtype)
    return out
```

```python
import numpy as np
import concourse.bass as bass
from concourse import mybir
from contextlib import ExitStack

FP32 = mybir.dt.float32
FP32R = mybir.dt.float32r
BF16 = mybir.dt.bfloat16
U32 = mybir.dt.uint32
ALU = mybir.AluOpType
ACT = mybir.ActivationFunctionType
AX = mybir.AxisListType

B, S, D = 8, 256, 1024
NQ, NKV, HD = 32, 8, 32
KV = NKV * HD
P = 128
G = NQ // NKV
PAIR = 2
T = PAIR * S
TT = T // P
KT = D // P
STEPS = B // PAIR
UNITS = NKV
SCALE = float(1.0 / np.sqrt(HD))
EPS = 1e-5
FP8_MAX = 448.0
MASKED = -1e30
ROWS = 3 * HD
HALF = 512

K_CHUNKS, V_CHUNKS, Q_CHUNKS, O_CHUNKS = KV // P, KV // P, UNITS, 2 * KT // 2
ATTN_CHUNKS = K_CHUNKS + V_CHUNKS + Q_CHUNKS + O_CHUNKS
CHUNKS = 2 * ATTN_CHUNKS + O_CHUNKS
RAW_RING, PART_RING = 3, 3

ACC = 4
TR = 2 * TT
USES = {}
_n = 0
for _name, _count in (("xT", TR), ("K0", K_CHUNKS), ("V0", TT), ("Q0", UNITS), ("O0", 2 * TT),
                      ("cT", TR), ("K1", K_CHUNKS), ("V1", TT), ("hT", TR), ("Q1", UNITS), ("O1", 2 * TT),
                      ("aT", TR), ("F", 2 * TT)):
    USES[_name] = _n
    _n += _count
ACC_USES = _n
TILES = K_CHUNKS + UNITS
ROUNDS = 2 * TT
STACKS = 3
FREE_STACKS = STACKS * ROUNDS

SLOT = KT
ROTATE, ROTATE2, LOW = 8, 9, 10
MAXES, MAX_T = 13, 21
SCORES = 24
PV = (29, 33)
DEN, NORM, NORM_LOW = 34, 35, 36
OUT0 = SLOT * UNITS
OUT_SLOTS = KT * TT
SLOTS = OUT0 + 2 * OUT_SLOTS + 1

USED_IN_ATTN = V_CHUNKS - 1 + 2 * (KT // 2 - 1)
USED = 2 * USED_IN_ATTN + 2 * (KT // 2 - 1)
STACK_DMAS = 3 * G
CONST_DMAS = 7
CONSTS = 10
START = 1
ACT_LINKS = 3 + 2 * UNITS
LN_LINKS = 6
QUANT_LINKS = 3 + 5 * TT
DVE_LINKS = 3 * LN_LINKS + QUANT_LINKS + TILES + 2 * 2 * UNITS


def decoder_layer(nc, x, ctx, wq1, wk1, wv1, wo1, wq2, bq2, wk2, bk2, wv2, bv2, wo2, bo2,
                  wf, wf_scale, cos_t, sin_t, out):
    stack = ExitStack()
    with stack:
        def sb(name, shape, dt):
            return stack.enter_context(nc.sbuf_tensor(name, shape, dt))

        def sem(name):
            return stack.enter_context(nc.semaphore(name))

        xres = sb("xres", [P, TT, D], FP32)
        ht = [sb(f"ht_{n}", [P, KT, T], FP32R) for n in ("hi", "lo")]
        kst = sb("kst", [P, NKV, T], FP32R)
        v_sb = sb("v_sb", [P, TT, KV], FP32)
        xn = nc.alloc_sbuf_tensor_at("xn", [P, TT, D], FP32, offset=nc.sbuf_base)
        qst = [sb(f"qst{i}", [P, G, T], FP32R) for i in range(STACKS)]
        rope_c = sb("rope_c", [P, T], FP32)
        rope_s = sb("rope_s", [P, T], FP32)
        part = [[sb(f"part_{n}{i}", [P, T], FP32R) for i in range(2)] for n in ("hi", "lo")]
        probs = sb("probs", [P, PAIR, 2, G, S], FP32)
        on = [sb(f"on_{n}", [P, UNITS, T], FP32R) for n in ("hi", "lo")]
        of = sb("of", [P, T], FP32)
        rden = sb("rden", [P, T], FP32)
        raw = [sb(f"raw{i}", [P, D], FP32) for i in range(RAW_RING)]
        wpart = [[sb(f"w_{n}{i}", [P, D], FP32R) for i in range(PART_RING)] for n in ("hi", "lo")]
        cos_sb = sb("cos_sb", [P, S], FP32)
        sin_sb = sb("sin_sb", [P, S], FP32)
        ident = sb("ident", [P, P], FP32)
        identb = sb("identb", [P, P], BF16)
        mask_qk = sb("mask_qk", [P, P], BF16)
        mask_kq = sb("mask_kq", [P, P], BF16)
        ones = sb("ones", [P, HD], FP32)
        bo_sb = sb("bo_sb", [P, D], FP32)
        bv_sb = sb("bv_sb", [P, KV], FP32)
        bq_sb = sb("bq_sb", [P, D // P], FP32)
        bk_sb = sb("bk_sb", [P, KV // P], FP32)
        ws_sb = sb("ws_sb", [P, KT * KT], FP32)
        stats = sb("stats", [P, TT, 2, 6], FP32)
        mv = sb("mv", [P, TT, 2], FP32)
        ve = sb("ve", [P, TT], FP32)
        lnv = sb("lnv", [P, TT], FP32)
        rs0 = sb("rs0", [P, TT], FP32)
        rs1 = sb("rs1", [P, TT], FP32)
        rstd = sb("rstd", [P, TT], FP32)
        mx = sb("mx", [P, G * TT], FP32)
        mneg = [sb(f"mneg{i}", [G, T], FP32R) for i in range(2)]
        amax = sb("amax", [P, TT * KT], FP32)
        qscale = sb("qscale", [P, TT * KT], FP32)
        rscale = sb("rscale", [P, TT * KT], FP32)
        flat = probs[:, :, :, :, :].rearrange("p b k g s -> p (b k g s)")
        ctx_sb = flat.rearrange("p (t d) -> p t d", t=TT)
        magic = ctx_sb

        acc = [stack.enter_context(nc.psum_tensor(f"acc{i}", [P, HALF], FP32)) for i in range(ACC)]
        mbank = stack.enter_context(nc.psum_tensor("mbank", [P, 2, S], FP32))
        sbank = stack.enter_context(nc.psum_tensor("sbank", [P, 2, S], FP32))
        obank = stack.enter_context(nc.psum_tensor("obank", [P, T], FP32))
        dbank = stack.enter_context(nc.psum_tensor("dbank", [P, T], FP32))

        wdt = nc.dram_tensor("wdt", (D, D), FP32, kind="Internal").ap()

        const_in = sem("const_in")
        consts = sem("consts")
        raw_in = [sem(f"raw_in{i}") for i in range(RAW_RING)]
        split_done = sem("split_done")
        chunk_used = sem("chunk_used")
        acc_full = sem("acc_full")
        acc_out = sem("acc_out")
        x_in = sem("x_in")
        ctx_in = sem("ctx_in")
        out_done = sem("out_done")
        var_ready = sem("var_ready")
        rs_ready = sem("rs_ready")
        xn_ready = sem("xn_ready")
        ht_hi = sem("ht_hi")
        rotated = sem("rotated")
        hi_ready = sem("hi_ready")
        lo_ready = sem("lo_ready")
        stacked = [sem(f"stacked{i}") for i in range(2)]
        max_full = sem("max_full")
        max_out = sem("max_out")
        mneg_in = [sem(f"mneg_in{i}") for i in range(2)]
        score_full = sem("score_full")
        exp_done = sem("exp_done")
        pv_done = sem("pv_done")
        den_ready = sem("den_ready")
        norm_done = sem("norm_done")
        on_hi = sem("on_hi")
        on_lo = sem("on_lo")
        bias_added = sem("bias_added")
        a_ready = sem("a_ready")
        vchain = sem("vchain")
        passed = sem("passed")
        achain = sem("achain")
        hi_split = sem("hi_split")
        wq_in = [sem(f"wq_in{i}") for i in range(2)]
        wq_scaled = sem("wq_scaled")
        wq_T = sem("wq_T")
        wq_out = sem("wq_out")
        wdt_stored = [sem(f"wdt_stored{i}") for i in range(2)]

        def kt_view(t, cols):
            return t[:, :].rearrange("p (k n) -> p k n", n=cols)

        def bank(use):
            return acc[use % ACC]

        def chunk_of(attn, name, i):
            start = {"K": 0, "V": K_CHUNKS, "Q": K_CHUNKS + V_CHUNKS, "O": ATTN_CHUNKS - O_CHUNKS}
            return attn * ATTN_CHUNKS + start[name] + i

        def chunk_source(c):
            if c >= 2 * ATTN_CHUNKS:
                w, i, kind = wdt, c - 2 * ATTN_CHUNKS, "O"
            else:
                a, i = divmod(c, ATTN_CHUNKS)
                wq, wk, wv, wo = ((wq1, wk1, wv1, wo1), (wq2, wk2, wv2, wo2))[a]
                if i < K_CHUNKS:
                    w, kind = wk, "K"
                elif i < K_CHUNKS + V_CHUNKS:
                    w, i, kind = wv, i - K_CHUNKS, "V"
                elif i < ATTN_CHUNKS - O_CHUNKS:
                    w, i, kind = wq, i - K_CHUNKS - V_CHUNKS, "K"
                else:
                    w, i, kind = wo, i - (ATTN_CHUNKS - O_CHUNKS), "O"
            rows = w.rearrange("(k p) n -> p k n", p=P)
            if kind == "K":
                return rows[:, :, i * P:(i + 1) * P]
            if kind == "V":
                return rows[:, i * 4:(i + 1) * 4, :]
            half, kp = divmod(i, KT // 2)
            return rows[:, 2 * kp:2 * kp + 2, half * HALF:(half + 1) * HALF]

        def slot_task(sl, offset, length=1):
            for u in range(UNITS):
                if 0 <= sl - SLOT * u - offset < length:
                    return u, sl - SLOT * u - offset
            return None

        def round_of(r):
            return r >> 2, (r >> 1) & 1, r & 1

        block = stack.enter_context(nc.Block())

        def drained(it, use):
            return it * ACC_USES + use + 1 + ACC

        def wait_chunk_used(engine, it, c):
            step, c = divmod(c, CHUNKS)
            a, i = divmod(c, ATTN_CHUNKS)
            o = i if a == 2 else i - (ATTN_CHUNKS - O_CHUNKS)
            counted = a * USED_IN_ATTN
            if o >= 0:
                half, kp = divmod(o, KT // 2)
                done = USES["F" if a == 2 else f"O{a}"] + (half + 1) * TT if kp == KT // 2 - 1 else None
                counted += (a < 2) + half * (KT // 2 - 1) + kp + 1
            elif i < K_CHUNKS:
                done = USES[f"K{a}"] + i + 1
            elif i == K_CHUNKS:
                done = None
                counted += 1
            elif i == K_CHUNKS + 1:
                done = USES[f"V{a}"] + TT
            else:
                done = USES[f"Q{a}"] + i - K_CHUNKS - V_CHUNKS + 1
            if done is None:
                engine.wait_ge(chunk_used, it * USED + step * USED + counted + PART_RING)
            else:
                engine.wait_ge(acc_full, it * ACC_USES + step * ACC_USES + done + START)

        def split_of(it, c):
            return it * CHUNKS + c + 1 + RAW_RING

        def unit_of(it, attn, u):
            return it * 2 * UNITS + attn * UNITS + u

        def copies_of(it, attn, t):
            return (it * TILES + (attn * TILES + t) // 2 + 1) * STACK_DMAS * 16

        @block.sync
        def _(sp):
            w_rows = wf.rearrange("(n p) k -> n p k", p=P)
            for n in range(KT):
                if n >= 2:
                    sp.wait_ge(wq_T, n - 1)
                sp.dma_start(xn[:, n % 2, :], w_rows[n]).then_inc(wq_in[n % 2], 16)
            with sp.Fori(0, STEPS) as it:
                loaded = [0]

                def load_up_to(c):
                    while loaded[0] < min(c + 1, CHUNKS):
                        n = loaded[0]
                        sp.wait_ge(split_done, it * CHUNKS + n + 1)
                        if n == 2 * ATTN_CHUNKS:
                            for i in range(2):
                                sp.wait_ge(wdt_stored[i], 16 * KT // 2)
                        src = chunk_source(n)
                        dst = raw[n % RAW_RING][:, :].rearrange("p (k n) -> p k n", n=src.shape[2])
                        sp.dma_start(dst, src).then_inc(raw_in[n % RAW_RING], 16)
                        loaded[0] += 1

                def copy_stack(attn, t):
                    sp.wait_ge(lo_ready, it * 2 * TILES + attn * TILES + t + 1 + START)
                    if t < K_CHUNKS:
                        sp.wait_ge(score_full, unit_of(it, attn, 0) * ROUNDS + FREE_STACKS)
                        dst, h0, parts = kst, G * t, (0, 0, 1)
                    else:
                        u = t - K_CHUNKS
                        last = u - 3 if u >= 3 else (UNITS - 1 - (UNITS - 1 - u) % 3) - UNITS
                        sp.wait_ge(score_full, unit_of(it, attn, last + 1) * ROUNDS + FREE_STACKS)
                        dst, h0, parts = qst[u % 3], 0, (0, 1, 0)
                    for row, which in enumerate(parts):
                        for g in range(G):
                            sp.dma_start(dst[HD * row:HD * (row + 1), h0 + g, :].bitcast(FP32),
                                         part[which][t % 2][HD * g:HD * (g + 1), :].bitcast(FP32))\
                              .then_inc(stacked[t % 2], 16)

                def keys(attn):
                    load_up_to(chunk_of(attn, "V", 0) + 3)
                    for t in range(K_CHUNKS):
                        copy_stack(attn, t)

                def timeline(attn):
                    for sl in range(SLOTS):
                        load_up_to(chunk_of(attn, "Q", 0) + sl // SLOT + 3)
                        if (k := slot_task(sl, LOW)) is not None:
                            copy_stack(attn, K_CHUNKS + k[0])
                        if (k := slot_task(sl, MAX_T)) is not None:
                            u = k[0]
                            sp.wait_ge(max_out, unit_of(it, attn, u + 1) * (ROUNDS + 1) + START)
                            for g in range(G):
                                sp.dma_start(qst[u % STACKS][ROWS:ROWS + 1, g, :].bitcast(FP32),
                                             mneg[u % 2][g:g + 1, :].bitcast(FP32)).then_inc(mneg_in[u % 2], 16)
                        if attn == 0 and sl == OUT0 + OUT_SLOTS:
                            sp.wait_ge(pv_done, unit_of(it, 1, 0) * PAIR + PAIR)
                            for tt in range(TT):
                                sp.dma_start(ctx_sb[:, tt, :], ctx[it, tt, :, :]).then_inc(ctx_in, 16)

                for attn in range(2):
                    keys(attn)
                    timeline(attn)
                load_up_to(CHUNKS - 1)

        @block.gpsimd
        def _(pool):
            made = [0]

            def step(instruction):
                made[0] += 1
                instruction.then_inc(consts, 1)
                pool.wait_ge(consts, made[0])

            for m in (ident, identb):
                step(nc.gpsimd.memset(m[:, :], 0.0))
                step(nc.gpsimd.affine_select(out=m[:, :], in_=m[:, :], compare_op=ALU.not_equal, fill=1.0,
                                             base=0, pattern=[[-1, P]], channel_multiplier=1))
            for m, by_key, by_row in ((mask_qk, -1, 1), (mask_kq, 1, -1)):
                step(nc.gpsimd.memset(m[:, :], 0.0))
                step(nc.gpsimd.affine_select(out=m[:, :], in_=m[:, :], compare_op=ALU.is_ge, fill=MASKED,
                                             base=0, pattern=[[by_key, P]], channel_multiplier=by_row))
            step(nc.gpsimd.memset(ones[:, :], 1.0))
            step(nc.gpsimd.memset(kst[ROWS:ROWS + 1, :, :].bitcast(FP32), 1.0))
            pool.sem_inc(split_done, RAW_RING)
            with pool.Fori(0, STEPS) as it:
                for c in range(CHUNKS):
                    r, hi, lo = raw[c % RAW_RING], wpart[0][c % PART_RING], wpart[1][c % PART_RING]
                    pool.wait_ge(raw_in[c % RAW_RING], (it * (CHUNKS // RAW_RING) + c // RAW_RING + 1) * 16)
                    wait_chunk_used(pool, it, c - PART_RING)
                    pool.sem_inc(passed, 1)
                    nc.gpsimd.tensor_copy(hi[:, :], r[:, :]).then_inc(hi_split, 1)
                    pool.wait_ge(hi_split, it * CHUNKS + c + 1)
                    nc.gpsimd.tensor_tensor(lo[:, :], r[:, :], hi[:, :].bitcast(FP32), ALU.subtract)\
                      .then_inc(split_done, 1)
                    if c == chunk_of(1, "Q", 2):
                        pool.wait_ge(xn_ready, it * 3 * TT + 2 * TT)
                        pool.wait_ge(const_in, CONST_DMAS * 16)
                        for tt in range(TT):
                            added = nc.gpsimd.tensor_tensor(xres[:, tt, :], xres[:, tt, :], bo_sb[:, :], ALU.add)
                        added.then_inc(bias_added, 1)

        @block.scalar
        def _(act):
            for dst, src in ((cos_sb[:, :], cos_t), (sin_sb[:, :], sin_t),
                             (bo_sb[:, :], bo2.unsqueeze(0).to_broadcast([P, D])),
                             (bv_sb[:, :], bv2.unsqueeze(0).to_broadcast([P, KV])),
                             (bq_sb[:, :], bq2.rearrange("(c p) -> p c", p=P)),
                             (bk_sb[:, :], bk2.rearrange("(c p) -> p c", p=P)),
                             (ws_sb[:, :], wf_scale.rearrange("n k -> (n k)").unsqueeze(0)
                              .to_broadcast([P, KT * KT]))):
                act.dma_start(dst, src, allow_slow_non_contiguous=True).then_inc(const_in, 16)
            wdt_rows = wdt.rearrange("(k p) n -> p k n", p=P)
            for n in range(KT):
                act.wait_ge(wq_T, n + 1)
                if n >= 2:
                    act.wait_ge(wdt_stored[n % 2], 16 * (n // 2))
                for j in range(2):
                    copied = nc.scalar.activation(ctx_sb[:, n % 2, j * HALF:(j + 1) * HALF],
                                                  acc[2 * (n % 2) + j][:, :], ACT.Copy)
                copied.then_inc(wq_out, 1)
                act.wait_ge(wq_out, n + 1)
                act.dma_start(wdt_rows[:, :, n * P:(n + 1) * P],
                              ctx_sb[:, n % 2, :].rearrange("p (k n) -> p k n", n=P))\
                   .then_inc(wdt_stored[n % 2], 16)
            for i in range(2):
                act.wait_ge(wdt_stored[i], 16 * KT // 2)
            for s in (exp_done, out_done, stacked[0], stacked[1]):
                act.sem_inc(s, START)
            with act.Fori(0, STEPS) as it:
                links = [0]

                def link(instruction):
                    links[0] += 1
                    instruction.then_inc(achain, 1)
                    act.wait_ge(achain, it * ACT_LINKS + links[0])

                def rsqrt_guess(n):
                    act.wait_ge(var_ready, it * 3 + n + 1)
                    link(nc.scalar.activation(lnv[:, :], ve[:, :], ACT.Ln))
                    nc.scalar.activation(rs0[:, :], lnv[:, :], ACT.Exp, scale=-0.5).then_inc(rs_ready, 1)

                def transposed_high(name):
                    for i in range(TR):
                        tt, half = divmod(i, 2)
                        act.wait_ge(acc_full, it * ACC_USES + USES[name] + i + 1 + START)
                        nc.scalar.activation(
                            ht[0][:, half * 4:half * 4 + 4, tt * P:(tt + 1) * P],
                            bank(USES[name] + i)[:, :].rearrange("p (k t) -> p k t", t=P),
                            ACT.Copy).then_inc(ht_hi, 1)

                def tile_high(attn, t):
                    act.wait_ge(rotated, it * 2 * TILES + attn * TILES + t + 1)
                    act.wait_ge(stacked[t % 2], copies_of(it, attn, t) - STACK_DMAS * 16 + START)
                    nc.scalar.activation(part[0][t % 2][:, :], rope_c[:, :], ACT.Copy).then_inc(hi_ready, 1)

                def keys(attn):
                    for t in range(K_CHUNKS):
                        tile_high(attn, t)

                def timeline(attn):
                    causal = attn == 0
                    for sl in range(SLOTS):
                        if (k := slot_task(sl, SCORES, ROUNDS)) is not None:
                            u, r = k
                            b, kt, hp = round_of(r)
                            q0 = kt * P if causal else 0
                            if r % 4 == 0:
                                act.wait_ge(pv_done, unit_of(it, attn, u) * PAIR + b + 1)
                            act.wait_ge(score_full, unit_of(it, attn, u) * ROUNDS + r + 1 + FREE_STACKS)
                            nc.scalar.activation(probs[:, b, kt, 2 * hp:2 * hp + 2, q0:S],
                                                 sbank[:, :, q0:S], ACT.Exp, scale=SCALE)\
                              .then_inc(exp_done, 1)
                        if (k := slot_task(sl, ROTATE2)) is not None:
                            tile_high(attn, K_CHUNKS + k[0])
                        if (k := slot_task(sl, DEN)) is not None:
                            u = k[0]
                            act.wait_ge(pv_done, unit_of(it, attn, u + 1) * PAIR + PAIR)
                            act.wait_ge(norm_done, unit_of(it, attn, u) + START)
                            link(nc.scalar.activation(rden[:, :], dbank[:, :], ACT.Ln))
                            nc.scalar.activation(rden[:, :], rden[:, :], ACT.Exp, scale=-1.0)\
                              .then_inc(den_ready, 1)
                        if (k := slot_task(sl, NORM)) is not None:
                            u = k[0]
                            act.wait_ge(norm_done, unit_of(it, attn, u + 1) + START)
                            nc.scalar.activation(on[0][:, u, :], of[:, :], ACT.Copy).then_inc(on_hi, 1)

                act.wait_ge(out_done, it * TT * 16 + START)
                for tt in range(TT):
                    act.dma_start(xres[:, tt, :], x[it, tt, :, :]).then_inc(x_in, 16)
                rsqrt_guess(0)
                transposed_high("xT")
                keys(0)
                timeline(0)
                transposed_high("cT")
                rsqrt_guess(1)
                keys(1)
                transposed_high("hT")
                timeline(1)
                rsqrt_guess(2)
                transposed_high("aT")
                for tt in range(TT):
                    act.wait_ge(acc_out, drained(it, USES["F"] + TT + tt))
                    act.dma_start(out[it, tt, :, :], xres[:, tt, :]).then_inc(out_done, 16)
                assert links[0] == ACT_LINKS
            act.wait_ge(out_done, STEPS * TT * 16 + START)

        @block.vector
        def _(dve):
            dve.wait_ge(const_in, CONST_DMAS * 16)
            for n in range(KT):
                dve.wait_ge(wq_in[n % 2], 16 * (n // 2 + 1))
                rows = xn[:, n % 2, :].rearrange("p (k c) -> p k c", c=P)
                nc.vector.tensor_tensor(rows, rows, ws_sb[:, n * KT:(n + 1) * KT].unsqueeze(2)
                                        .to_broadcast([P, KT, P]), ALU.mult).then_inc(wq_scaled, 1)
            dve.wait_ge(wq_T, KT)
            dve.sem_inc(acc_out, ACC)
            for s in (max_out, norm_done, on_lo, lo_ready, mneg_in[0], mneg_in[1]):
                dve.sem_inc(s, START)
            with dve.Fori(0, STEPS) as it:
                links = [0]

                def link(instruction):
                    links[0] += 1
                    instruction.then_inc(vchain, 1)
                    dve.wait_ge(vchain, it * DVE_LINKS + links[0])

                def layer_norm(n):
                    for tt in range(TT):
                        for h in range(2):
                            last = nc.vector.bn_stats(stats[:, tt, h, :], xres[:, tt, h * HALF:(h + 1) * HALF])
                    link(last)
                    dve.sem_inc(passed, 1)
                    for tt in range(TT):
                        last = nc.vector.bn_aggr(mv[:, tt, :], stats[:, tt, :, :].rearrange("p h s -> p (h s)"))
                    link(last)
                    nc.vector.tensor_scalar(ve[:, :], mv[:, :, 1], EPS, None, ALU.add).then_inc(var_ready, 1)
                    dve.wait_ge(var_ready, it * 3 + n + 1)
                    dve.wait_ge(rs_ready, it * 3 + n + 1)
                    link(nc.vector.tensor_tensor(rs1[:, :], rs0[:, :], rs0[:, :], ALU.mult))
                    link(nc.vector.tensor_tensor(rs1[:, :], rs1[:, :], ve[:, :], ALU.mult))
                    link(nc.vector.tensor_scalar(rs1[:, :], rs1[:, :], -0.5, 1.5, ALU.mult, ALU.add))
                    link(nc.vector.tensor_tensor(rstd[:, :], rs0[:, :], rs1[:, :], ALU.mult))
                    for tt in range(TT):
                        nc.vector.tensor_scalar(xn[:, tt, :], xres[:, tt, :], mv[:, tt, 0:1], rstd[:, tt:tt + 1],
                                                ALU.subtract, ALU.mult).then_inc(xn_ready, 1)

                def transposed_low(name, n):
                    for i in range(TR):
                        tt, half = divmod(i, 2)
                        at = (slice(None), slice(half * 4, half * 4 + 4), slice(tt * P, (tt + 1) * P))
                        dve.wait_ge(ht_hi, it * 4 * TR + n * TR + i + 1)
                        nc.vector.tensor_tensor(
                            ht[1][at], bank(USES[name] + i)[:, :].rearrange("p (k t) -> p k t", t=P),
                            ht[0][at].bitcast(FP32), ALU.subtract).then_inc(acc_out, 1)

                def tile_rotate(attn, t):
                    use = USES[f"K{attn}"] + t if t < K_CHUNKS else USES[f"Q{attn}"] + t - K_CHUNKS
                    dve.wait_ge(acc_full, it * ACC_USES + use + 1 + START)
                    dve.wait_ge(lo_ready, it * 2 * TILES + attn * TILES + t + START)
                    if attn == 0:
                        dve.sem_inc(passed, 1)
                        nc.vector.stream_shuffle(rope_s[:, :], bank(use)[:, :],
                                                 [(i + HD // 2) % HD for i in range(HD)])
                        nc.vector.tensor_tensor(
                            rope_c[:, :].rearrange("p (b s) -> p b s", s=S),
                            bank(use)[:, :].rearrange("p (b s) -> p b s", s=S),
                            cos_sb[:, :].unsqueeze(1).to_broadcast([P, PAIR, S]), ALU.mult).then_inc(acc_out, 1)
                    else:
                        bias = bk_sb[:, t:t + 1] if t < K_CHUNKS else bq_sb[:, t - K_CHUNKS:t - K_CHUNKS + 1]
                        nc.vector.tensor_scalar(rope_c[:, :], bank(use)[:, :], bias, None, ALU.add)\
                          .then_inc(acc_out, 1)

                def tile_rotate2(attn, t):
                    use = USES[f"K{attn}"] + t if t < K_CHUNKS else USES[f"Q{attn}"] + t - K_CHUNKS
                    dve.wait_ge(acc_out, drained(it, use))
                    if attn == 0:
                        link(nc.vector.tensor_tensor(
                            rope_s[:, :].rearrange("p (b s) -> p b s", s=S),
                            rope_s[:, :].rearrange("p (b s) -> p b s", s=S),
                            sin_sb[:, :].unsqueeze(1).to_broadcast([P, PAIR, S]), ALU.mult))
                        nc.vector.tensor_tensor(rope_c[:, :], rope_c[:, :], rope_s[:, :], ALU.add)\
                          .then_inc(rotated, 1)
                    else:
                        dve.sem_inc(rotated, 1)

                def tile_low(attn, t):
                    dve.wait_ge(hi_ready, it * 2 * TILES + attn * TILES + t + 1)
                    nc.vector.tensor_tensor(part[1][t % 2][:, :], rope_c[:, :],
                                            part[0][t % 2][:, :].bitcast(FP32), ALU.subtract)\
                      .then_inc(lo_ready, 1)

                def keys_values(attn):
                    for t in range(K_CHUNKS):
                        tile_rotate(attn, t)
                        tile_rotate2(attn, t)
                        tile_low(attn, t)
                    for tt in range(TT):
                        use = USES[f"V{attn}"] + tt
                        dve.wait_ge(acc_full, it * ACC_USES + use + 1 + START)
                        if attn == 0:
                            copied = nc.vector.tensor_copy(v_sb[:, tt, :], bank(use)[:, 0:KV])
                        else:
                            copied = nc.vector.tensor_tensor(v_sb[:, tt, :], bank(use)[:, 0:KV], bv_sb[:, :], ALU.add)
                        copied.then_inc(acc_out, 1)

                def add_output(name, half):
                    for tt in range(TT):
                        use = USES[name] + half * TT + tt
                        dve.wait_ge(acc_full, it * ACC_USES + use + 1 + START)
                        to = xres[:, tt, half * HALF:(half + 1) * HALF]
                        nc.vector.tensor_tensor(to, bank(use)[:, :], to, ALU.add).then_inc(acc_out, 1)

                def timeline(attn):
                    causal = attn == 0
                    for sl in range(SLOTS):
                        if (k := slot_task(sl, MAX_T)) is not None:
                            u = k[0]
                            dve.wait_ge(max_full, unit_of(it, attn, u + 1) * (ROUNDS + 1))
                            dve.wait_ge(mneg_in[u % 2], (it * UNITS + (attn * UNITS + u) // 2) * G * 16 + START)
                            nc.vector.tensor_scalar(mneg[u % 2][:, :], mbank[0:G, :, :].rearrange("p h s -> p (h s)"), -1.0, None,
                                                    ALU.mult).then_inc(max_out, 1)
                        if (k := slot_task(sl, MAXES, ROUNDS)) is not None:
                            u, r = k
                            b, qt, hp = round_of(r)
                            nk = (qt + 1) * P if causal else S
                            dve.wait_ge(max_full, unit_of(it, attn, u) * (ROUNDS + 1) + r + 1)
                            nc.vector.reduce_max(
                                mx[:, (2 * b + qt) * G + 2 * hp:(2 * b + qt) * G + 2 * hp + 2],
                                mbank[:, :, 0:nk], AX.X).then_inc(max_out, 1)
                        if (k := slot_task(sl, ROTATE)) is not None:
                            tile_rotate(attn, K_CHUNKS + k[0])
                        if (k := slot_task(sl, ROTATE2)) is not None:
                            tile_rotate2(attn, K_CHUNKS + k[0])
                        if (k := slot_task(sl, LOW)) is not None:
                            tile_low(attn, K_CHUNKS + k[0])
                        if (k := slot_task(sl, NORM)) is not None:
                            u = k[0]
                            dve.wait_ge(den_ready, unit_of(it, attn, u + 1))
                            dve.wait_ge(on_lo, unit_of(it, attn, u) + START)
                            link(nc.vector.tensor_tensor(of[:, :], dbank[:, :], rden[:, :], ALU.mult))
                            link(nc.vector.scalar_tensor_tensor(rden[:, :], of[:, :], 2.0, rden[:, :],
                                                                ALU.subtract, ALU.mult))
                            nc.vector.scalar_tensor_tensor(of[:, :], obank[:, :], -1.0, rden[:, :],
                                                           ALU.mult, ALU.mult).then_inc(norm_done, 1)
                        if (k := slot_task(sl, NORM_LOW)) is not None:
                            u = k[0]
                            dve.wait_ge(on_hi, unit_of(it, attn, u + 1))
                            nc.vector.tensor_tensor(on[1][:, u, :], of[:, :], on[0][:, u, :].bitcast(FP32),
                                                    ALU.subtract).then_inc(on_lo, 1)
                        for half in range(2):
                            if sl == OUT0 + (half + 1) * OUT_SLOTS:
                                if attn == 1:
                                    dve.wait_ge(bias_added, it + 1)
                                add_output(f"O{attn}", half)

                def quantise():
                    dve.wait_ge(xn_ready, (it + 1) * 3 * TT)
                    for tt in range(TT):
                        last = nc.vector.tensor_reduce(amax[:, tt * KT:(tt + 1) * KT],
                                                       xn[:, tt, :].rearrange("p (k c) -> p k c", c=P),
                                                       AX.X, ALU.max, apply_absolute_value=True)
                    link(last)
                    link(nc.vector.tensor_scalar(qscale[:, :], amax[:, :], 1.0 / FP8_MAX, None, ALU.mult))
                    link(nc.vector.reciprocal(rscale[:, :], qscale[:, :]))
                    for tt in range(TT):
                        v, m = xn[:, tt, :], magic[:, tt, :]
                        blocks = v.rearrange("p (k c) -> p k c", c=P)

                        def of_block(s):
                            return s[:, tt * KT:(tt + 1) * KT].unsqueeze(2).to_broadcast([P, KT, P])

                        link(nc.vector.tensor_tensor(blocks, blocks, of_block(rscale), ALU.mult))
                        link(nc.vector.tensor_scalar(m.bitcast(U32), v.bitcast(U32), 0x7F800000, None,
                                                     ALU.bitwise_and))
                        link(nc.vector.tensor_scalar(m, m, 2.0 ** -6, 1.5 * 2.0 ** 20, ALU.max, ALU.mult))
                        link(nc.vector.tensor_tensor(v, v, m, ALU.add))
                        link(nc.vector.tensor_tensor(v, v, m, ALU.subtract))
                        nc.vector.tensor_tensor(blocks, blocks, of_block(qscale), ALU.mult).then_inc(a_ready, 1)

                dve.wait_ge(x_in, (it + 1) * TT * 16)
                layer_norm(0)
                transposed_low("xT", 0)
                keys_values(0)
                timeline(0)
                transposed_low("cT", 1)
                dve.wait_ge(acc_out, drained(it, USES["O0"] + 2 * TT - 1))
                layer_norm(1)
                keys_values(1)
                transposed_low("hT", 2)
                timeline(1)
                dve.wait_ge(acc_out, drained(it, USES["O1"] + 2 * TT - 1))
                layer_norm(2)
                quantise()
                transposed_low("aT", 3)
                for half in range(2):
                    add_output("F", half)
                assert links[0] == DVE_LINKS, links[0]

        @block.tensor
        def _(pe):
            pe.wait_ge(consts, CONSTS)
            for n in range(KT):
                pe.wait_ge(wq_scaled, n + 1)
                if n >= 2:
                    pe.wait_ge(wq_out, n - 1)
                for k in range(KT):
                    last = nc.tensor.transpose(acc[2 * (n % 2) + k // 4][:, (k % 4) * P:(k % 4 + 1) * P],
                                               xn[:, n % 2, k * P:(k + 1) * P], ident[:, :])
                last.then_inc(wq_T, 1)
            pe.wait_ge(wq_out, KT)
            pe.sem_inc(chunk_used, PART_RING)
            pe.sem_inc(pv_done, PAIR)
            pe.sem_inc(score_full, FREE_STACKS)
            pe.sem_inc(acc_full, START)
            with pe.Fori(0, STEPS) as it:

                def product(dst, left, right, first, last):
                    nc.tensor.matmul(dst, left[0], right[0], start=first, stop=False)
                    nc.tensor.matmul(dst, left[1], right[0], start=False, stop=False)
                    return nc.tensor.matmul(dst, left[0], right[1], start=False, stop=last)

                def take_bank(use):
                    pe.wait_ge(acc_out, it * ACC_USES + use + 1)
                    return bank(use)

                def weights(c, cols):
                    pe.wait_ge(split_done, split_of(it, c))
                    return [kt_view(wpart[i][c % PART_RING], cols) for i in range(2)]

                def transpose_in(name, tile, ready):
                    for i in range(TR):
                        tt, half = divmod(i, 2)
                        if half == 0:
                            ready(tt)
                        dst = take_bank(USES[name] + i)
                        for j in range(4):
                            k = half * 4 + j
                            last = nc.tensor.transpose(dst[:, j * P:(j + 1) * P], tile[:, tt, k * P:(k + 1) * P],
                                                       ident[:, :])
                        last.then_inc(acc_full, 1)

                def project_tile(dst, w, k):
                    return product(dst[:, :], [w[i][:, k, :] for i in range(2)], [ht[i][:, k, :] for i in range(2)],
                                   k == 0, k == KT - 1)

                def keys_values(attn, name):
                    pe.wait_ge(acc_out, drained(it, USES[name] + TR - 1))
                    for t in range(K_CHUNKS):
                        c = chunk_of(attn, "K", t)
                        w = weights(c, P)
                        dst = take_bank(USES[f"K{attn}"] + t)
                        for k in range(KT):
                            last = project_tile(dst, w, k)
                        last.then_inc(acc_full, 1)
                    for i in range(V_CHUNKS):
                        c = chunk_of(attn, "V", i)
                        w = weights(c, KV)
                        for tt in range(TT):
                            use = USES[f"V{attn}"] + tt
                            dst = take_bank(use) if i == 0 else bank(use)
                            for kk in range(4):
                                k = i * 4 + kk
                                last = product(dst[:, 0:KV], [ht[j][:, k, tt * P:(tt + 1) * P] for j in range(2)],
                                               [w[j][:, kk, :] for j in range(2)], k == 0, k == KT - 1)
                            if i == V_CHUNKS - 1:
                                last.then_inc(acc_full, 1)
                        if i < V_CHUNKS - 1:
                            last.then_inc(chunk_used, 1)

                def output_step(name, c0, left, half, k, tt):
                    c = c0 + half * (KT // 2) + k // 2
                    w = weights(c, HALF) if k % 2 == 0 and tt == 0 else [kt_view(wpart[i][c % PART_RING], HALF)
                                                                         for i in range(2)]
                    use = USES[name] + half * TT + tt
                    dst = take_bank(use) if k == 0 else bank(use)
                    last = product(dst[:, :], [left[i][:, k, tt * P:(tt + 1) * P] for i in range(2)],
                                   [w[i][:, k % 2, :] for i in range(2)], k == 0, k == KT - 1)
                    if k == KT - 1:
                        last.then_inc(acc_full, 1)
                    elif k % 2 == 1 and tt == TT - 1:
                        last.then_inc(chunk_used, 1)

                def max_round(attn, u, r):
                    causal = attn == 0
                    b, qt, hp = round_of(r)
                    nk = (qt + 1) * P if causal else S
                    if r == 0:
                        pe.wait_ge(stacked[0], copies_of(it, attn, (K_CHUNKS + u) // 2 * 2) + START)
                        pe.wait_ge(stacked[1], copies_of(it, attn, (K_CHUNKS + u - 1) // 2 * 2 + 1) + START)
                    pe.wait_ge(max_out, unit_of(it, attn, u) * (ROUNDS + 1) + r + START)
                    for h in range(2):
                        last = nc.tensor.matmul(mbank[:, h, 0:nk],
                                                qst[u % STACKS][0:ROWS, 2 * hp + h, (2 * b + qt) * P:(2 * b + qt + 1) * P],
                                                kst[0:ROWS, u, b * S:b * S + nk], start=True, stop=not causal)
                        if causal:
                            last = nc.tensor.matmul(mbank[:, h, qt * P:(qt + 1) * P], identb[:, :], mask_qk[:, :],
                                                    start=False, stop=True)
                    last.then_inc(max_full, 1)

                def transpose_maxima(attn, u):
                    pe.wait_ge(max_out, unit_of(it, attn, u) * (ROUNDS + 1) + ROUNDS + START)
                    for tt in range(TT):
                        last = nc.tensor.transpose(mbank[0:G, tt // 2, (tt % 2) * P:(tt % 2 + 1) * P],
                                                   mx[:, tt * G:(tt + 1) * G], ident[:, :])
                    last.then_inc(max_full, 1)

                def score_round(attn, u, r):
                    causal = attn == 0
                    b, kt, hp = round_of(r)
                    q0 = kt * P if causal else 0
                    if r == 0:
                        pe.wait_ge(mneg_in[u % 2], (it * UNITS + (attn * UNITS + u) // 2 + 1) * G * 16 + START)
                    pe.wait_ge(exp_done, unit_of(it, attn, u) * ROUNDS + r + START)
                    last = nc.tensor.matmul(sbank[:, :, q0:S], kst[0:ROWS + 1, u, b * S + kt * P:b * S + (kt + 1) * P],
                                            qst[u % STACKS][0:ROWS + 1, 2 * hp:2 * hp + 2, b * S + q0:(b + 1) * S],
                                            start=True, stop=not causal)
                    if causal:
                        last = nc.tensor.matmul(sbank[:, :, q0:q0 + P], identb[:, :],
                                                mask_kq[:, :].unsqueeze(1).to_broadcast([P, 2, P]),
                                                start=False, stop=True)
                    last.then_inc(score_full, 1)

                def pv(attn, u, b):
                    if u == 0:
                        pe.wait_ge(acc_out, drained(it, USES[f"V{attn}"] + TT - 1))
                    pe.wait_ge(exp_done, unit_of(it, attn, u) * ROUNDS + (b + 1) * TT + START)
                    if b == 0:
                        pe.wait_ge(norm_done, unit_of(it, attn, u) + START)
                    for dst, left in ((obank, lambda kt: v_sb[:, 2 * b + kt, HD * u:HD * (u + 1)]),
                                      (dbank, lambda kt: ones[:, :])):
                        for kt in range(2):
                            q0 = kt * P if attn == 0 else 0
                            for g in range(G):
                                last = nc.tensor.matmul(dst[HD * g:HD * (g + 1), b * S + q0:(b + 1) * S], left(kt),
                                                        probs[:, b, kt, g, q0:S], start=kt == 0, stop=kt == 1,
                                                        tile_position=(0, HD * g))
                    last.then_inc(pv_done, 1)

                def timeline(attn):
                    for sl in range(SLOTS):
                        if (k := slot_task(sl, 0, SLOT)) is not None:
                            u, kt = k
                            c = chunk_of(attn, "Q", u)
                            if kt == 0:
                                wq = weights(c, P)
                                dst = take_bank(USES[f"Q{attn}"] + u)
                            last = project_tile(dst, wq, kt)
                            if kt == KT - 1:
                                last.then_inc(acc_full, 1)
                        elif sl < OUT0 + 2 * OUT_SLOTS:
                            half, rest = divmod(sl - OUT0, OUT_SLOTS)
                            k, tt = divmod(rest, TT)
                            if half == 0 and tt == 0:
                                pe.wait_ge(on_lo, unit_of(it, attn, k + 1) + START)
                            output_step(f"O{attn}", chunk_of(attn, "O", 0), on, half, k, tt)
                        for b in range(PAIR):
                            if (k := slot_task(sl, PV[b])) is not None:
                                pv(attn, k[0], b)
                        if (k := slot_task(sl, MAX_T)) is not None:
                            transpose_maxima(attn, k[0])
                        if (k := slot_task(sl, MAXES, ROUNDS)) is not None:
                            max_round(attn, *k)
                        if (k := slot_task(sl, SCORES, ROUNDS)) is not None:
                            score_round(attn, *k)

                transpose_in("xT", xn, lambda tt: pe.wait_ge(xn_ready, it * 3 * TT + tt + 1))
                keys_values(0, "xT")
                timeline(0)
                pe.wait_ge(ctx_in, (it + 1) * TT * 16)
                transpose_in("cT", ctx_sb, lambda tt: None)
                keys_values(1, "cT")
                transpose_in("hT", xn, lambda tt: pe.wait_ge(xn_ready, it * 3 * TT + TT + tt + 1))
                pe.wait_ge(acc_out, drained(it, USES["hT"] + TR - 1))
                timeline(1)
                transpose_in("aT", xn, lambda tt: pe.wait_ge(a_ready, it * TT + tt + 1))
                pe.wait_ge(acc_out, drained(it, USES["aT"] + TR - 1))
                for half in range(2):
                    for k in range(KT):
                        for tt in range(TT):
                            output_step("F", 2 * ATTN_CHUNKS, ht, half, k, tt)


_WEIGHTS = ["L0_attn_Wq", "L0_attn_Wk", "L0_attn_Wv", "L0_attn_Wo", "L0_xattn_Wq", "L0_xattn_bq", "L0_xattn_Wk",
            "L0_xattn_bk", "L0_xattn_Wv", "L0_xattn_bv", "L0_xattn_Wo", "L0_xattn_bo", "L0_ffn_weight",
            "L0_ffn_weight_scale"]


def rope_tables():
    inv = (np.float32(1.0) / np.float32(10000.0) ** (np.arange(0, HD, 2, dtype=np.float32) / np.float32(HD)))
    freqs = np.arange(S, dtype=np.float32)[:, None] * inv.astype(np.float32)[None, :]
    cos, sin = np.cos(freqs).astype(np.float32).T, np.sin(freqs).astype(np.float32).T
    return (np.ascontiguousarray(np.tile(np.concatenate([cos, cos]), (G, 1))),
            np.ascontiguousarray(np.tile(np.concatenate([-sin, sin]), (G, 1))))


def kernel(**inputs):
    import concourse.bacc as _bacc
    from concourse.bass_utils import run_bass_kernel_spmd as _run

    nc = _bacc.Bacc("TRN2", target_bir_lowering=False, num_devices=1)
    arrays, args = {}, []
    cos, sin = rope_tables()
    host = [("x", np.ascontiguousarray(inputs["x"]).reshape(STEPS, TT, P, D)),
            ("ctx", np.ascontiguousarray(inputs["ctx_4096"]).reshape(STEPS, TT, P, D))]
    host += [(name, np.ascontiguousarray(inputs[name])) for name in _WEIGHTS]
    host += [("cos", cos), ("sin", sin)]
    for name, a in host:
        arrays[f"in_{name}"] = a
        args.append(nc.dram_tensor(f"in_{name}", a.shape, mybir.dt.from_np(a.dtype), kind="ExternalInput").ap())
    args.append(nc.dram_tensor("out_x", (STEPS, TT, P, D), FP32, kind="ExternalOutput").ap())
    decoder_layer(nc, *args)
    r = _run(nc, [arrays], core_ids=[0])
    return r.results[0]["out_x"].reshape(B, S, D)
```

```python
import numpy as np
import concourse.bass as bass
from concourse import mybir
from contextlib import ExitStack

FP32 = mybir.dt.float32
FP32R = mybir.dt.float32r
BF16 = mybir.dt.bfloat16
U32 = mybir.dt.uint32
ALU = mybir.AluOpType
ACT = mybir.ActivationFunctionType
AX = mybir.AxisListType

B, S, D = 8, 256, 1024
NQ, NKV, HD = 32, 8, 32
KV = NKV * HD
P = 128
G = NQ // NKV
PAIR = 2
T = PAIR * S
TT = T // P
KT = D // P
STEPS = B // PAIR
UNITS = NKV
SCALE = float(1.0 / np.sqrt(HD))
EPS = 1e-5
FP8_MAX = 448.0
MASKED = -1e30
EXP_AND_LN = 6
ROWS = 3 * HD
HALF = 512

def numbered(*groups):
    first, n = {}, 0
    for name, count in groups:
        first[name] = n
        n += count
    return first, n


K_CHUNKS, V_CHUNKS, O_CHUNKS = KV // P, KV // P, KT
CHUNK, CHUNKS = numbered(("Q0", UNITS), ("O0", O_CHUNKS), ("K1", K_CHUNKS), ("V1", V_CHUNKS), ("Q1", UNITS),
                         ("O1", O_CHUNKS), ("K0", K_CHUNKS), ("V0", V_CHUNKS), ("F", O_CHUNKS))
RAW_RING, PART_RING = 3, 3
ACC = 4
TR = 2 * TT
USES, ACC_USES = numbered(("Q0", UNITS), ("O0", 2 * TT), ("cT", TR), ("K1", K_CHUNKS), ("V1", TT), ("hT", TR),
                          ("Q1", UNITS), ("O1", 2 * TT), ("xT", TR), ("K0", K_CHUNKS), ("V0", TT), ("aT", TR),
                          ("F", 2 * TT))
TRANSPOSED, _ = numbered(("cT", TR), ("hT", TR), ("xT", TR), ("aT", TR))
TILE, TILES = numbered(("Q0", UNITS), ("K1", K_CHUNKS), ("Q1", UNITS), ("K0", K_CHUNKS))
LN, LNS = numbered(("cross", 1), ("next", 1), ("ffn", 1))
ROUNDS = 2 * TT
STACKS = 4
FREE_STACKS = STACKS * ROUNDS

SLOT = KT
ROTATE, ROTATE2, HIGH, LOW = 8, 9, 10, 11
MAXES, MAX_T = 20, 28
SCORES = 35
PV, SUMS = (SCORES + 6, SCORES + 8), (SCORES + 7, SCORES + 9)
DEN, REFINE, NORM, NORM_HIGH, NORM_LOW = (SUMS[1] + _i for _i in (0, 1, 2, 3, 4))
OUT_AT = []
for _k in range(KT):
    OUT_AT.append(max(OUT_AT[-1] + TT if OUT_AT else SLOT * UNITS, SLOT * _k + NORM_LOW + 1))
OUT_AT += [OUT_AT[-1] + TT * (_k + 1) for _k in range(KT)]
OUT_DONE = (OUT_AT[KT], OUT_AT[-1] + TT)
LOAD_AT = SLOT * (UNITS - 1) + SUMS[1] + 1
NORM_AT = OUT_DONE[0] + 1
SLOTS = OUT_DONE[1] + 1

STACK_DMAS = 3 * G
CONST_DMAS = 6
CONSTS = 10
START = 1
ACT_LINKS = LNS + 2 * UNITS
LN_LINKS = 6
QUANT_LINKS = 3 + 5 * TT
DVE_LINKS = LNS * LN_LINKS + QUANT_LINKS + UNITS + K_CHUNKS + 2 * 2 * UNITS


def decoder_layer(nc, x, ctx, wq1, wk1, wv1, wo1, wq2, bq2, wk2, bk2, wv2, bv2, wo2, bo2,
                  wf, wf_scale, cos_t, sin_t, out):
    stack = ExitStack()
    with stack:
        def sb(name, shape, dt):
            return stack.enter_context(nc.sbuf_tensor(name, shape, dt))

        def sem(name):
            return stack.enter_context(nc.semaphore(name))

        xres = sb("xres", [P, TT, D], FP32)
        ht = [sb(f"ht_{n}", [P, KT, T], FP32R) for n in ("hi", "lo")]
        kst = sb("kst", [P, NKV, T], FP32R)
        v_sb = sb("v_sb", [P, TT, KV], FP32)
        xn = nc.alloc_sbuf_tensor_at("xn", [P, TT, D], FP32, offset=nc.sbuf_base)
        qst = [sb(f"qst{i}", [P, G, T], FP32R) for i in range(STACKS)]
        rope_c = sb("rope_c", [P, T], FP32)
        rope_s = sb("rope_s", [P, T], FP32)
        part = [[sb(f"part_{n}{i}", [P, T], FP32R) for i in range(2)] for n in ("hi", "lo")]
        probs = sb("probs", [P, PAIR, 2, G, S], FP32)
        on_hi_sb = sb("on_hi", [P, UNITS, T], FP32R)
        of = nc.alloc_sbuf_tensor_at("of", [P, UNITS, T], FP32, offset=nc.sbuf_base)
        on = [on_hi_sb, sb("on_lo", [P, UNITS, T], FP32R)]
        rden = sb("rden", [P, T], FP32)
        raw = [sb(f"raw{i}", [P, D], FP32) for i in range(RAW_RING)]
        wpart = [[sb(f"w_{n}{i}", [P, D], FP32R) for i in range(PART_RING)] for n in ("hi", "lo")]
        cos_sb = sb("cos_sb", [P, S], FP32)
        sin_sb = sb("sin_sb", [P, S], FP32)
        ident = sb("ident", [P, P], FP32)
        identb = sb("identb", [P, P], BF16)
        mask_qk = sb("mask_qk", [P, P], BF16)
        mask_kq = sb("mask_kq", [P, P], BF16)
        ones = sb("ones", [P, HD], FP32)
        bv_sb = sb("bv_sb", [P, KV], FP32)
        bq_sb = sb("bq_sb", [P, D // P], FP32)
        bk_sb = sb("bk_sb", [P, KV // P], FP32)
        ws_sb = sb("ws_sb", [P, KT * KT], FP32)
        stats = [sb(f"stats{i}", [P, TT, 2, 6], FP32) for i in range(2)]
        mv = sb("mv", [P, TT, 2], FP32)
        ve = sb("ve", [P, TT], FP32)
        lnv = sb("lnv", [P, TT], FP32)
        rs0 = sb("rs0", [P, TT], FP32)
        rs1 = sb("rs1", [P, TT], FP32)
        rstd = sb("rstd", [P, TT], FP32)
        mx = sb("mx", [P, G * TT], FP32)
        mneg = [sb(f"mneg{i}", [G, T], FP32R) for i in range(2)]
        amax = sb("amax", [P, TT * KT], FP32)
        qscale = sb("qscale", [P, TT * KT], FP32)
        rscale = sb("rscale", [P, TT * KT], FP32)
        flat = probs[:, :, :, :, :].rearrange("p b k g s -> p (b k g s)")
        ctx_sb = flat.rearrange("p (t d) -> p t d", t=TT)
        magic = ctx_sb
        next_x = ctx_sb
        bo_sb = of[:, UNITS - 2:UNITS, :].rearrange("p u n -> p (u n)")

        acc = [stack.enter_context(nc.psum_tensor(f"acc{i}", [P, HALF], FP32)) for i in range(ACC)]
        mbank = stack.enter_context(nc.psum_tensor("mbank", [P, 2, S], FP32))
        sbank = stack.enter_context(nc.psum_tensor("sbank", [P, 2, S], FP32))
        obank = stack.enter_context(nc.psum_tensor("obank", [P, T], FP32))
        dbank = stack.enter_context(nc.psum_tensor("dbank", [P, T], FP32))

        wdt = nc.dram_tensor("wdt", (D, D), FP32, kind="Internal").ap()

        const_in = sem("const_in")
        consts = sem("consts")
        raw_in = [sem(f"raw_in{i}") for i in range(RAW_RING)]
        split_done = sem("split_done")
        chunk_begun = sem("chunk_begun")
        acc_full = sem("acc_full")
        acc_out = sem("acc_out")
        xres_in = sem("xres_in")
        next_in = sem("next_in")
        bo_in = sem("bo_in")
        ctx_in = sem("ctx_in")
        out_done = sem("out_done")
        var_ready = sem("var_ready")
        rs_ready = sem("rs_ready")
        xn_ready = sem("xn_ready")
        ht_hi = sem("ht_hi")
        rotated = sem("rotated")
        hi_ready = sem("hi_ready")
        lo_ready = sem("lo_ready")
        stacked = [sem(f"stacked{i}") for i in range(2)]
        max_full = sem("max_full")
        max_out = sem("max_out")
        mneg_in = [sem(f"mneg_in{i}") for i in range(2)]
        score_full = sem("score_full")
        exp_done = sem("exp_done")
        pv_done = sem("pv_done")
        den_ready = sem("den_ready")
        norm_done = sem("norm_done")
        on_hi = sem("on_hi")
        on_lo = sem("on_lo")
        bias_added = sem("bias_added")
        a_ready = sem("a_ready")
        vchain = sem("vchain")
        passed = sem("passed")
        achain = sem("achain")
        hi_split = sem("hi_split")
        wq_in = [sem(f"wq_in{i}") for i in range(2)]
        wq_scaled = sem("wq_scaled")
        wq_T = sem("wq_T")
        wq_out = sem("wq_out")
        wdt_stored = [sem(f"wdt_stored{i}") for i in range(2)]

        def kt_view(t, cols):
            return t[:, :].rearrange("p (k n) -> p k n", n=cols)

        def bank(use):
            return acc[use % ACC]

        def chunk_source(c):
            name, first = [(n, f) for n, f in CHUNK.items() if f <= c][-1]
            i = c - first
            w = {"K0": wk1, "V0": wv1, "Q0": wq1, "O0": wo1, "K1": wk2, "V1": wv2, "Q1": wq2, "O1": wo2,
                 "F": wdt}[name]
            rows = w.rearrange("(k p) n -> p k n", p=P)
            if name[0] in "KQ":
                return rows[:, :, i * P:(i + 1) * P]
            if name[0] == "V":
                return rows[:, i * 4:(i + 1) * 4, :]
            half, kp = divmod(i, KT // 2)
            return rows[:, 2 * kp:2 * kp + 2, half * HALF:(half + 1) * HALF]

        def slot_task(sl, offset, length=1):
            for u in range(UNITS):
                if 0 <= sl - SLOT * u - offset < length:
                    return u, sl - SLOT * u - offset
            return None

        def round_of(r):
            return r >> 2, (r >> 1) & 1, r & 1

        block = stack.enter_context(nc.Block())

        def filled(it, use):
            return (it + 1) * ACC_USES + use + 1

        def drained(it, use):
            return (it + 1) * ACC_USES + use + 1

        def split_of(it, c):
            return (it + 1) * CHUNKS + c + 1

        def unit_of(it, attn, u):
            return it * 2 * UNITS + attn * UNITS + u

        def tile_count(it, t):
            return (it + 1) * TILES + t + 1

        def copies_of(it, t):
            return ((it + 1) * (TILES // 2) + t // 2 + 1) * STACK_DMAS * 16

        def ln_count(it, name):
            return (it + 1) * LNS + LN[name] + 1

        def normalised(it, name, tt):
            return ((it + 1) * LNS + LN[name]) * TT + tt + 1

        def add_credit(engine, semaphore, value):
            while value > 0:
                engine.sem_inc(semaphore, min(value, 240))
                value -= 240

        @block.sync
        def _(sp):
            w_rows = wf.rearrange("(n p) k -> n p k", p=P)
            for n in range(KT):
                if n >= 2:
                    sp.wait_ge(wq_T, n - 1)
                sp.dma_start(xn[:, n % 2, :], w_rows[n]).then_inc(wq_in[n % 2], 16)
            loaded = [0]

            def load_up_to(it, c):
                while loaded[0] <= c:
                    n = loaded[0]
                    sp.wait_ge(split_done, split_of(it, n - RAW_RING))
                    if n == CHUNK["F"]:
                        for i in range(2):
                            sp.wait_ge(wdt_stored[i], 16 * KT // 2)
                    src = chunk_source(n)
                    dst = raw[n % RAW_RING][:, :].rearrange("p (k n) -> p k n", n=src.shape[2])
                    sp.dma_start(dst, src).then_inc(raw_in[n % RAW_RING], 16)
                    loaded[0] += 1

            def copy_stack(it, name, i, which):
                t = TILE[name] + i
                sp.wait_ge((hi_ready, lo_ready)[which], tile_count(it, t))
                if name[0] == "K":
                    sp.wait_ge(score_full, unit_of(it, 1, 0 if name == "K1" else UNITS) * ROUNDS + FREE_STACKS)
                    dst, h0, rows = kst, G * i, ((0, 1), (2,))[which]
                else:
                    sp.wait_ge(score_full, unit_of(it, int(name[1]), i - STACKS + 1) * ROUNDS + FREE_STACKS)
                    dst, h0, rows = qst[i % STACKS], 0, ((0, 2), (1,))[which]
                for row in rows:
                    for g in range(G):
                        sp.dma_start(dst[HD * row:HD * (row + 1), h0 + g, :].bitcast(FP32),
                                     part[which][t % 2][HD * g:HD * (g + 1), :].bitcast(FP32))\
                          .then_inc(stacked[t % 2], 16)

            def keys(it, attn, ahead):
                load_up_to(it, CHUNK[f"V{attn}"] + V_CHUNKS - 1 + ahead)
                for i in range(K_CHUNKS):
                    for which in range(2):
                        copy_stack(it, f"K{attn}", i, which)

            def timeline(it, attn):
                for sl in range(SLOTS):
                    load_up_to(it, min(CHUNK[f"Q{attn}"] + sl // SLOT + 3, CHUNK[f"O{attn}"] + O_CHUNKS - 1))
                    if (k := slot_task(sl, HIGH)) is not None:
                        copy_stack(it, f"Q{attn}", k[0], 0)
                    if (k := slot_task(sl, LOW)) is not None:
                        copy_stack(it, f"Q{attn}", k[0], 1)
                    if (k := slot_task(sl, MAX_T)) is not None:
                        u = k[0]
                        sp.wait_ge(max_out, unit_of(it, attn, u + 1) * (ROUNDS + 1) + START)
                        for g in range(G):
                            sp.dma_start(qst[u % STACKS][ROWS:ROWS + 1, g, :].bitcast(FP32),
                                         mneg[u % 2][g:g + 1, :].bitcast(FP32)).then_inc(mneg_in[u % 2], 16)
                    if attn == 0 and sl == 2 * SLOT:
                        sp.wait_ge(out_done, it * TT * 16 + START)
                        for tt in range(TT):
                            sp.dma_start(xres[:, tt, :], x[it, tt, :, :]).then_inc(xres_in, 16)
                    if sl == LOAD_AT:
                        sp.wait_ge(pv_done, unit_of(it, attn + 1, 0) * PAIR + PAIR)
                        for tt in range(TT):
                            if attn == 0:
                                sp.dma_start(ctx_sb[:, tt, :], ctx[it, tt, :, :]).then_inc(ctx_in, 16)
                            else:
                                sp.dma_start(next_x[:, tt, :], x[1:, :, :, :][it, tt, :, :])\
                                  .then_inc(next_in, 16)

            for i in range(2):
                sp.wait_ge(wdt_stored[i], 16 * KT // 2)
            for tt in range(TT):
                sp.dma_start(next_x[:, tt, :], x[0, tt, :, :]).then_inc(next_in, 16)
            for s, n in ((raw_in[i], CHUNK["K0"] // RAW_RING) for i in range(RAW_RING)):
                add_credit(sp, s, 16 * n)
            loaded[0] = CHUNK["K0"]
            keys(-1, 0, 0)
            for i in range(RAW_RING):
                skipped = len([c for c in range(CHUNK["F"], CHUNKS) if c % RAW_RING == i])
                sp.wait_ge(split_done, split_of(-1, CHUNK["F"] - 1))
                add_credit(sp, raw_in[i], 16 * skipped)
            with sp.Fori(0, STEPS) as it:
                loaded[0] = 0
                timeline(it, 0)
                load_up_to(it, CHUNK["V1"] + V_CHUNKS - 1)
                sp.wait_ge(acc_full, filled(it, USES["O0"] + 2 * TT - 1))
                sp.dma_start(bo_sb, bo2.unsqueeze(0).to_broadcast([P, D])).then_inc(bo_in, 16)
                keys(it, 1, 2)
                timeline(it, 1)
                keys(it, 0, 2)
                load_up_to(it, CHUNKS - 1)

        @block.gpsimd
        def _(pool):
            made = [0]

            def step(instruction):
                made[0] += 1
                instruction.then_inc(consts, 1)
                pool.wait_ge(consts, made[0])

            for m in (ident, identb):
                step(nc.gpsimd.memset(m[:, :], 0.0))
                step(nc.gpsimd.affine_select(out=m[:, :], in_=m[:, :], compare_op=ALU.not_equal, fill=1.0,
                                             base=0, pattern=[[-1, P]], channel_multiplier=1))
            for m, by_key, by_row in ((mask_qk, -1, 1), (mask_kq, 1, -1)):
                step(nc.gpsimd.memset(m[:, :], 0.0))
                step(nc.gpsimd.affine_select(out=m[:, :], in_=m[:, :], compare_op=ALU.is_ge, fill=MASKED,
                                             base=0, pattern=[[by_key, P]], channel_multiplier=by_row))
            step(nc.gpsimd.memset(ones[:, :], 1.0))
            step(nc.gpsimd.memset(kst[ROWS:ROWS + 1, :, :].bitcast(FP32), 1.0))
            def split(it, c):
                r, hi, lo = raw[c % RAW_RING], wpart[0][c % PART_RING], wpart[1][c % PART_RING]
                pool.wait_ge(raw_in[c % RAW_RING], ((it + 1) * (CHUNKS // RAW_RING) + c // RAW_RING + 1) * 16)
                pool.wait_ge(chunk_begun, (it + 1) * CHUNKS + c - PART_RING + 2)
                pool.sem_inc(passed, 1)
                nc.gpsimd.tensor_copy(hi[:, :], r[:, :]).then_inc(hi_split, 1)
                pool.wait_ge(hi_split, (it + 1) * CHUNKS + c + 1)
                nc.gpsimd.tensor_tensor(lo[:, :], r[:, :], hi[:, :].bitcast(FP32), ALU.subtract)\
                  .then_inc(split_done, 1)

            for s in (hi_split, split_done):
                pool.sem_inc(s, CHUNK["K0"])
            for c in range(CHUNK["K0"], CHUNK["F"]):
                split(-1, c)
            pool.wait_ge(split_done, split_of(-1, CHUNK["F"] - 1))
            for s in (hi_split, split_done):
                pool.sem_inc(s, CHUNKS - CHUNK["F"])
            with pool.Fori(0, STEPS) as it:
                for c in range(CHUNKS):
                    split(it, c)
                    if c == CHUNK["Q1"] + 2:
                        pool.wait_ge(xn_ready, normalised(it, "cross", TT - 1))
                        pool.wait_ge(bo_in, (it + 1) * 16)
                        for tt in range(TT):
                            added = nc.gpsimd.tensor_tensor(xres[:, tt, :], xres[:, tt, :], bo_sb, ALU.add)
                        added.then_inc(bias_added, 1)

        @block.scalar
        def _(act):
            act.add_instruction(mybir.InstLoadActFuncSet(name=nc.get_next_instruction_name(), ins=[], outs=[],
                                                         act_func_set_id=EXP_AND_LN))
            for dst, src in ((cos_sb[:, :], cos_t), (sin_sb[:, :], sin_t),
                             (bv_sb[:, :], bv2.unsqueeze(0).to_broadcast([P, KV])),
                             (bq_sb[:, :], bq2.rearrange("(c p) -> p c", p=P)),
                             (bk_sb[:, :], bk2.rearrange("(c p) -> p c", p=P)),
                             (ws_sb[:, :], wf_scale.rearrange("n k -> (n k)").unsqueeze(0)
                              .to_broadcast([P, KT * KT]))):
                act.dma_start(dst, src, allow_slow_non_contiguous=True).then_inc(const_in, 16)
            wdt_rows = wdt.rearrange("(k p) n -> p k n", p=P)
            for n in range(KT):
                act.wait_ge(wq_T, n + 1)
                if n >= 2:
                    act.wait_ge(wdt_stored[n % 2], 16 * (n // 2))
                for j in range(2):
                    copied = nc.scalar.activation(ctx_sb[:, n % 2, j * HALF:(j + 1) * HALF],
                                                  acc[2 * (n % 2) + j][:, :], ACT.Copy)
                copied.then_inc(wq_out, 1)
                act.wait_ge(wq_out, n + 1)
                act.dma_start(wdt_rows[:, :, n * P:(n + 1) * P],
                              ctx_sb[:, n % 2, :].rearrange("p (k n) -> p k n", n=P))\
                   .then_inc(wdt_stored[n % 2], 16)
            def link(instruction):
                links[0] += 1
                instruction.then_inc(achain, 1)
                act.wait_ge(achain, links[0] + base[0])

            def rsqrt_guess(it, name):
                act.wait_ge(var_ready, ln_count(it, name))
                link(nc.scalar.activation(lnv[:, :], ve[:, :], ACT.Ln))
                nc.scalar.activation(rs0[:, :], lnv[:, :], ACT.Exp, scale=-0.5).then_inc(rs_ready, 1)

            def transposed_high(it, name, to):
                for i in range(TR):
                    tt, half = divmod(i, 2)
                    act.wait_ge(acc_full, filled(it, USES[name] + i))
                    nc.scalar.activation(
                        to[0][:, half * 4:half * 4 + 4, tt * P:(tt + 1) * P],
                        bank(USES[name] + i)[:, :].rearrange("p (k t) -> p k t", t=P),
                        ACT.Copy).then_inc(ht_hi, 1)

            def tile_high(it, t):
                act.wait_ge(rotated, tile_count(it, t))
                act.wait_ge(stacked[t % 2], copies_of(it, t - 2))
                nc.scalar.activation(part[0][t % 2][:, :], rope_c[:, :], ACT.Copy).then_inc(hi_ready, 1)

            def keys(it, attn):
                for i in range(K_CHUNKS):
                    tile_high(it, TILE[f"K{attn}"] + i)

            def timeline(it, attn):
                causal = attn == 0
                for sl in range(SLOTS):
                    if (k := slot_task(sl, SCORES, ROUNDS)) is not None:
                        u, r = k
                        b, kt, hp = round_of(r)
                        q0 = kt * P if causal else 0
                        if r % 4 == 0:
                            act.wait_ge(pv_done, unit_of(it, attn, u) * PAIR + b + 1)
                        act.wait_ge(score_full, unit_of(it, attn, u) * ROUNDS + r + 1 + FREE_STACKS)
                        nc.scalar.activation(probs[:, b, kt, 2 * hp:2 * hp + 2, q0:S],
                                             sbank[:, :, q0:S], ACT.Exp, scale=SCALE)\
                          .then_inc(exp_done, 1)
                    if (k := slot_task(sl, HIGH)) is not None:
                        tile_high(it, TILE[f"Q{attn}"] + k[0])
                    if (k := slot_task(sl, DEN)) is not None:
                        u = k[0]
                        act.wait_ge(pv_done, unit_of(it, attn, u + 1) * PAIR + PAIR)
                        act.wait_ge(norm_done, unit_of(it, attn, u) + START)
                        link(nc.scalar.activation(rden[:, :], dbank[:, :], ACT.Ln))
                        nc.scalar.activation(rden[:, :], rden[:, :], ACT.Exp, scale=-1.0)\
                          .then_inc(den_ready, 1)
                    if (k := slot_task(sl, NORM_HIGH)) is not None:
                        u = k[0]
                        act.wait_ge(norm_done, unit_of(it, attn, u + 1) + START)
                        nc.scalar.activation(on[0][:, u, :], of[:, u, :], ACT.Copy).then_inc(on_hi, 1)
                    if attn == 1 and sl == NORM_AT:
                        rsqrt_guess(it, "next")

            links, base = [0], [0]
            for s in (exp_done, out_done):
                act.sem_inc(s, START)
            act.sem_inc(rs_ready, LN["next"])
            act.sem_inc(ht_hi, TRANSPOSED["xT"])
            act.sem_inc(hi_ready, TILE["K0"])
            rsqrt_guess(-1, "next")
            transposed_high(-1, "xT", ht)
            keys(-1, 0)
            act.wait_ge(ht_hi, TRANSPOSED["aT"])
            act.sem_inc(ht_hi, TR)
            act.sem_inc(rs_ready, LNS - LN["next"] - 1)
            act.sem_inc(achain, ACT_LINKS - links[0])
            with act.Fori(0, STEPS) as it:
                links[0], base[0] = 0, (it + 1) * ACT_LINKS
                timeline(it, 0)
                transposed_high(it, "cT", ht)
                rsqrt_guess(it, "cross")
                keys(it, 1)
                transposed_high(it, "hT", ht)
                timeline(it, 1)
                transposed_high(it, "xT", ht)
                rsqrt_guess(it, "ffn")
                keys(it, 0)
                transposed_high(it, "aT", on)
                for tt in range(TT):
                    act.wait_ge(acc_out, drained(it, USES["F"] + TT + tt))
                    act.dma_start(out[it, tt, :, :], xres[:, tt, :]).then_inc(out_done, 16)
                assert links[0] == ACT_LINKS
            act.wait_ge(out_done, STEPS * TT * 16 + START)

        @block.vector
        def _(dve):
            dve.wait_ge(const_in, CONST_DMAS * 16)
            for n in range(KT):
                dve.wait_ge(wq_in[n % 2], 16 * (n // 2 + 1))
                rows = xn[:, n % 2, :].rearrange("p (k c) -> p k c", c=P)
                nc.vector.tensor_tensor(rows, rows, ws_sb[:, n * KT:(n + 1) * KT].unsqueeze(2)
                                        .to_broadcast([P, KT, P]), ALU.mult).then_inc(wq_scaled, 1)
            dve.wait_ge(wq_T, KT)
            def link(instruction):
                links[0] += 1
                instruction.then_inc(vchain, 1)
                dve.wait_ge(vchain, links[0] + base[0])

            def statistics(of_x, half, which):
                for tt in range(TT):
                    last = nc.vector.bn_stats(stats[which][:, tt, half, :], of_x[:, tt, half * HALF:(half + 1) * HALF])
                return last

            def layer_norm(it, name, of_x, which):
                dve.sem_inc(passed, 1)
                for tt in range(TT):
                    last = nc.vector.bn_aggr(mv[:, tt, :], stats[which][:, tt, :, :].rearrange("p h s -> p (h s)"))
                link(last)
                nc.vector.tensor_scalar(ve[:, :], mv[:, :, 1], EPS, None, ALU.add).then_inc(var_ready, 1)
                dve.wait_ge(var_ready, ln_count(it, name))
                dve.wait_ge(rs_ready, ln_count(it, name))
                link(nc.vector.tensor_tensor(rs1[:, :], rs0[:, :], rs0[:, :], ALU.mult))
                link(nc.vector.tensor_tensor(rs1[:, :], rs1[:, :], ve[:, :], ALU.mult))
                link(nc.vector.tensor_scalar(rs1[:, :], rs1[:, :], -0.5, 1.5, ALU.mult, ALU.add))
                link(nc.vector.tensor_tensor(rstd[:, :], rs0[:, :], rs1[:, :], ALU.mult))
                for tt in range(TT):
                    nc.vector.tensor_scalar(xn[:, tt, :], of_x[:, tt, :], mv[:, tt, 0:1], rstd[:, tt:tt + 1],
                                            ALU.subtract, ALU.mult).then_inc(xn_ready, 1)

            def transposed_low(it, name, to):
                for i in range(TR):
                    tt, half = divmod(i, 2)
                    at = (slice(None), slice(half * 4, half * 4 + 4), slice(tt * P, (tt + 1) * P))
                    dve.wait_ge(ht_hi, ((it + 1) * 4 * TR + TRANSPOSED[name]) + i + 1)
                    nc.vector.tensor_tensor(
                        to[1][at], bank(USES[name] + i)[:, :].rearrange("p (k t) -> p k t", t=P),
                        to[0][at].bitcast(FP32), ALU.subtract).then_inc(acc_out, 1)

            def tile_rotate(it, name, i):
                t, use = TILE[name] + i, USES[name] + i
                dve.wait_ge(acc_full, filled(it, use))
                dve.wait_ge(lo_ready, tile_count(it, t - 1))
                if name[1] == "0":
                    dve.sem_inc(passed, 1)
                    nc.vector.stream_shuffle(rope_s[:, :], bank(use)[:, :], [(i + HD // 2) % HD for i in range(HD)])
                    nc.vector.tensor_tensor(
                        rope_c[:, :].rearrange("p (b s) -> p b s", s=S),
                        bank(use)[:, :].rearrange("p (b s) -> p b s", s=S),
                        cos_sb[:, :].unsqueeze(1).to_broadcast([P, PAIR, S]), ALU.mult).then_inc(acc_out, 1)
                else:
                    bias = (bk_sb if name == "K1" else bq_sb)[:, i:i + 1]
                    nc.vector.tensor_scalar(rope_c[:, :], bank(use)[:, :], bias, None, ALU.add)\
                      .then_inc(acc_out, 1)

            def tile_rotate2(it, name, i):
                dve.wait_ge(acc_out, drained(it, USES[name] + i))
                if name[1] == "0":
                    link(nc.vector.tensor_tensor(
                        rope_s[:, :].rearrange("p (b s) -> p b s", s=S),
                        rope_s[:, :].rearrange("p (b s) -> p b s", s=S),
                        sin_sb[:, :].unsqueeze(1).to_broadcast([P, PAIR, S]), ALU.mult))
                    nc.vector.tensor_tensor(rope_c[:, :], rope_c[:, :], rope_s[:, :], ALU.add)\
                      .then_inc(rotated, 1)
                else:
                    dve.sem_inc(rotated, 1)

            def tile_low(it, name, i):
                t = TILE[name] + i
                dve.wait_ge(hi_ready, tile_count(it, t))
                nc.vector.tensor_tensor(part[1][t % 2][:, :], rope_c[:, :],
                                        part[0][t % 2][:, :].bitcast(FP32), ALU.subtract).then_inc(lo_ready, 1)

            def keys(it, attn):
                for i in range(K_CHUNKS):
                    tile_rotate(it, f"K{attn}", i)
                    tile_rotate2(it, f"K{attn}", i)
                    tile_low(it, f"K{attn}", i)

            def values(it, attn):
                for tt in range(TT):
                    use = USES[f"V{attn}"] + tt
                    dve.wait_ge(acc_full, filled(it, use))
                    if attn == 0:
                        dve.wait_ge(pv_done, unit_of(it, 1, UNITS) * PAIR + PAIR)
                        copied = nc.vector.tensor_copy(v_sb[:, tt, :], bank(use)[:, 0:KV])
                    else:
                        copied = nc.vector.tensor_tensor(v_sb[:, tt, :], bank(use)[:, 0:KV], bv_sb[:, :], ALU.add)
                    copied.then_inc(acc_out, 1)

            def add_output(it, name, half):
                for tt in range(TT):
                    use = USES[name] + half * TT + tt
                    dve.wait_ge(acc_full, filled(it, use))
                    to = xres[:, tt, half * HALF:(half + 1) * HALF]
                    nc.vector.tensor_tensor(to, bank(use)[:, :], to, ALU.add).then_inc(acc_out, 1)

            def timeline(it, attn):
                causal = attn == 0
                for sl in range(SLOTS):
                    if (k := slot_task(sl, MAX_T)) is not None:
                        u = k[0]
                        dve.wait_ge(max_full, unit_of(it, attn, u + 1) * (ROUNDS + 1))
                        dve.wait_ge(mneg_in[u % 2], (it * UNITS + (attn * UNITS + u) // 2) * G * 16 + START)
                        nc.vector.tensor_scalar(mneg[u % 2][:, :], mbank[0:G, :, :].rearrange("p h s -> p (h s)"), -1.0, None,
                                                ALU.mult).then_inc(max_out, 1)
                    if (k := slot_task(sl, MAXES, ROUNDS)) is not None:
                        u, r = k
                        b, qt, hp = round_of(r)
                        nk = (qt + 1) * P if causal else S
                        dve.wait_ge(max_full, unit_of(it, attn, u) * (ROUNDS + 1) + r + 1)
                        nc.vector.reduce_max(
                            mx[:, (2 * b + qt) * G + 2 * hp:(2 * b + qt) * G + 2 * hp + 2],
                            mbank[:, :, 0:nk], AX.X).then_inc(max_out, 1)
                    if (k := slot_task(sl, ROTATE)) is not None:
                        tile_rotate(it, f"Q{attn}", k[0])
                    if (k := slot_task(sl, ROTATE2)) is not None:
                        tile_rotate2(it, f"Q{attn}", k[0])
                    if (k := slot_task(sl, LOW)) is not None:
                        tile_low(it, f"Q{attn}", k[0])
                    if (k := slot_task(sl, REFINE)) is not None:
                        u = k[0]
                        dve.wait_ge(den_ready, unit_of(it, attn, u + 1))
                        if attn == 1 and u == UNITS - 2:
                            dve.wait_ge(bias_added, it + 1)
                        o = of[:, u, :]
                        link(nc.vector.tensor_tensor(o, dbank[:, :], rden[:, :], ALU.mult))
                        link(nc.vector.scalar_tensor_tensor(rden[:, :], o, 2.0, rden[:, :],
                                                            ALU.subtract, ALU.mult))
                    if (k := slot_task(sl, NORM)) is not None:
                        o = of[:, k[0], :]
                        nc.vector.scalar_tensor_tensor(o, obank[:, :], -1.0, rden[:, :],
                                                       ALU.mult, ALU.mult).then_inc(norm_done, 1)
                    if (k := slot_task(sl, NORM_LOW)) is not None:
                        u = k[0]
                        dve.wait_ge(on_hi, unit_of(it, attn, u + 1))
                        nc.vector.tensor_tensor(on[1][:, u, :], of[:, u, :], on[0][:, u, :].bitcast(FP32),
                                                ALU.subtract).then_inc(on_lo, 1)
                    for half in range(2):
                        if sl == OUT_DONE[half]:
                            if attn == 0 and half == 0:
                                dve.wait_ge(xres_in, (it + 1) * TT * 16)
                            add_output(it, f"O{attn}", half)
                            dve.wait_ge(acc_out, drained(it, USES[f"O{attn}"] + half * TT + TT - 1))
                            last = statistics(xres, half, 0)
                            if half == 1:
                                link(last)
                    if attn == 1 and sl == NORM_AT:
                        normalise_next(it)

            def normalise_next(it):
                dve.wait_ge(next_in, (it + 2) * TT * 16)
                statistics(next_x, 0, 1)
                link(statistics(next_x, 1, 1))
                dve.wait_ge(score_full, unit_of(it, 1, UNITS) * ROUNDS + FREE_STACKS)
                layer_norm(it, "next", next_x, 1)

            def quantise(it):
                dve.wait_ge(xn_ready, normalised(it, "ffn", TT - 1))
                for tt in range(TT):
                    last = nc.vector.tensor_reduce(amax[:, tt * KT:(tt + 1) * KT],
                                                   xn[:, tt, :].rearrange("p (k c) -> p k c", c=P),
                                                   AX.X, ALU.max, apply_absolute_value=True)
                link(last)
                link(nc.vector.tensor_scalar(qscale[:, :], amax[:, :], 1.0 / FP8_MAX, None, ALU.mult))
                link(nc.vector.reciprocal(rscale[:, :], qscale[:, :]))
                values(it, 0)
                for tt in range(TT):
                    v, m = xn[:, tt, :], magic[:, tt, :]
                    blocks = v.rearrange("p (k c) -> p k c", c=P)

                    def of_block(s):
                        return s[:, tt * KT:(tt + 1) * KT].unsqueeze(2).to_broadcast([P, KT, P])

                    link(nc.vector.tensor_tensor(blocks, blocks, of_block(rscale), ALU.mult))
                    link(nc.vector.tensor_scalar(m.bitcast(U32), v.bitcast(U32), 0x7F800000, None,
                                                 ALU.bitwise_and))
                    link(nc.vector.tensor_scalar(m, m, 2.0 ** -6, 1.5 * 2.0 ** 20, ALU.max, ALU.mult))
                    link(nc.vector.tensor_tensor(v, v, m, ALU.add))
                    link(nc.vector.tensor_tensor(v, v, m, ALU.subtract))
                    nc.vector.tensor_tensor(blocks, blocks, of_block(qscale), ALU.mult).then_inc(a_ready, 1)

            links, base = [0], [0]
            for s in (max_out, norm_done, on_lo, mneg_in[0], mneg_in[1]):
                dve.sem_inc(s, START)
            dve.sem_inc(acc_out, USES["xT"])
            dve.sem_inc(var_ready, LN["next"])
            dve.sem_inc(xn_ready, LN["next"] * TT)
            for s in (rotated, lo_ready):
                dve.sem_inc(s, TILE["K0"])
            for i in range(2):
                add_credit(dve, stacked[i], copies_of(-1, TILE["K0"] + i - 2))
            normalise_next(-1)
            transposed_low(-1, "xT", ht)
            keys(-1, 0)
            values(-1, 0)
            dve.wait_ge(acc_out, drained(-1, USES["V0"] + TT - 1))
            dve.sem_inc(acc_out, ACC_USES - USES["aT"])
            dve.sem_inc(var_ready, LNS - LN["next"] - 1)
            dve.sem_inc(xn_ready, (LNS - LN["next"] - 1) * TT)
            dve.sem_inc(vchain, DVE_LINKS - links[0])
            with dve.Fori(0, STEPS) as it:
                links[0], base[0] = 0, (it + 1) * DVE_LINKS
                timeline(it, 0)
                transposed_low(it, "cT", ht)
                layer_norm(it, "cross", xres, 0)
                keys(it, 1)
                values(it, 1)
                transposed_low(it, "hT", ht)
                timeline(it, 1)
                transposed_low(it, "xT", ht)
                layer_norm(it, "ffn", xres, 0)
                keys(it, 0)
                quantise(it)
                transposed_low(it, "aT", on)
                for half in range(2):
                    add_output(it, "F", half)
                assert links[0] == DVE_LINKS, links[0]

        @block.tensor
        def _(pe):
            pe.wait_ge(consts, CONSTS)
            for n in range(KT):
                pe.wait_ge(wq_scaled, n + 1)
                if n >= 2:
                    pe.wait_ge(wq_out, n - 1)
                for k in range(KT):
                    last = nc.tensor.transpose(acc[2 * (n % 2) + k // 4][:, (k % 4) * P:(k % 4 + 1) * P],
                                               xn[:, n % 2, k * P:(k + 1) * P], ident[:, :])
                last.then_inc(wq_T, 1)
            pe.wait_ge(wq_out, KT)
            def product(dst, left, right, first, last, begins):
                high = nc.tensor.matmul(dst, left[0], right[0], start=first, stop=False)
                if begins:
                    high.then_inc(chunk_begun, 1)
                nc.tensor.matmul(dst, left[1], right[0], start=False, stop=False)
                return nc.tensor.matmul(dst, left[0], right[1], start=False, stop=last)

            def take_bank(it, use):
                pe.wait_ge(acc_out, drained(it, use - ACC))
                return bank(use)

            def weights(it, c, cols):
                pe.wait_ge(split_done, split_of(it, c))
                return [kt_view(wpart[i][c % PART_RING], cols) for i in range(2)]

            def transpose_in(it, name, tile, ready):
                for i in range(TR):
                    tt, half = divmod(i, 2)
                    if half == 0:
                        ready(tt)
                    dst = take_bank(it, USES[name] + i)
                    for j in range(4):
                        k = half * 4 + j
                        last = nc.tensor.transpose(dst[:, j * P:(j + 1) * P], tile[:, tt, k * P:(k + 1) * P],
                                                   ident[:, :])
                    last.then_inc(acc_full, 1)

            def project_tile(dst, w, k):
                return product(dst[:, :], [w[i][:, k, :] for i in range(2)], [ht[i][:, k, :] for i in range(2)],
                               k == 0, k == KT - 1, k == 0)

            def keys_values(it, attn, name):
                pe.wait_ge(acc_out, drained(it, USES[name] + TR - 1))
                for t in range(K_CHUNKS):
                    w = weights(it, CHUNK[f"K{attn}"] + t, P)
                    dst = take_bank(it, USES[f"K{attn}"] + t)
                    for k in range(KT):
                        last = project_tile(dst, w, k)
                    last.then_inc(acc_full, 1)
                for i in range(V_CHUNKS):
                    w = weights(it, CHUNK[f"V{attn}"] + i, KV)
                    for tt in range(TT):
                        use = USES[f"V{attn}"] + tt
                        dst = take_bank(it, use) if i == 0 else bank(use)
                        for kk in range(4):
                            k = i * 4 + kk
                            last = product(dst[:, 0:KV], [ht[j][:, k, tt * P:(tt + 1) * P] for j in range(2)],
                                           [w[j][:, kk, :] for j in range(2)], k == 0, k == KT - 1,
                                           tt == 0 and kk == 0)
                        if i == V_CHUNKS - 1:
                            last.then_inc(acc_full, 1)

            def output_step(it, name, left, half, k, tt):
                c = CHUNK[name] + half * (KT // 2) + k // 2
                w = weights(it, c, HALF) if k % 2 == 0 and tt == 0 else [kt_view(wpart[i][c % PART_RING], HALF)
                                                                     for i in range(2)]
                use = USES[name] + half * TT + tt
                dst = take_bank(it, use) if k == 0 else bank(use)
                last = product(dst[:, :], [left[i][:, k, tt * P:(tt + 1) * P] for i in range(2)],
                               [w[i][:, k % 2, :] for i in range(2)], k == 0, k == KT - 1,
                               k % 2 == 0 and tt == 0)
                if k == KT - 1:
                    last.then_inc(acc_full, 1)

            def max_round(it, attn, u, r):
                causal = attn == 0
                b, qt, hp = round_of(r)
                nk = (qt + 1) * P if causal else S
                if r == 0:
                    for t in (TILE[f"Q{attn}"] + u, TILE[f"Q{attn}"] + u - 1):
                        pe.wait_ge(stacked[t % 2], copies_of(it, t))
                pe.wait_ge(max_out, unit_of(it, attn, u) * (ROUNDS + 1) + r + START)
                for h in range(2):
                    last = nc.tensor.matmul(mbank[:, h, 0:nk],
                                            qst[u % STACKS][0:ROWS, 2 * hp + h, (2 * b + qt) * P:(2 * b + qt + 1) * P],
                                            kst[0:ROWS, u, b * S:b * S + nk], start=True, stop=not causal)
                    if causal:
                        last = nc.tensor.matmul(mbank[:, h, qt * P:(qt + 1) * P], identb[:, :], mask_qk[:, :],
                                                start=False, stop=True)
                last.then_inc(max_full, 1)

            def transpose_maxima(it, attn, u):
                pe.wait_ge(max_out, unit_of(it, attn, u) * (ROUNDS + 1) + ROUNDS + START)
                for tt in range(TT):
                    last = nc.tensor.transpose(mbank[0:G, tt // 2, (tt % 2) * P:(tt % 2 + 1) * P],
                                               mx[:, tt * G:(tt + 1) * G], ident[:, :])
                last.then_inc(max_full, 1)

            def score_round(it, attn, u, r):
                causal = attn == 0
                b, kt, hp = round_of(r)
                q0 = kt * P if causal else 0
                if r == 0:
                    pe.wait_ge(mneg_in[u % 2], (it * UNITS + (attn * UNITS + u) // 2 + 1) * G * 16 + START)
                pe.wait_ge(exp_done, unit_of(it, attn, u) * ROUNDS + r + START)
                last = nc.tensor.matmul(sbank[:, :, q0:S], kst[0:ROWS + 1, u, b * S + kt * P:b * S + (kt + 1) * P],
                                        qst[u % STACKS][0:ROWS + 1, 2 * hp:2 * hp + 2, b * S + q0:(b + 1) * S],
                                        start=True, stop=not causal)
                if causal:
                    last = nc.tensor.matmul(sbank[:, :, q0:q0 + P], identb[:, :],
                                            mask_kq[:, :].unsqueeze(1).to_broadcast([P, 2, P]),
                                            start=False, stop=True)
                last.then_inc(score_full, 1)

            def pv(it, attn, u, b):
                if u == 0:
                    pe.wait_ge(acc_out, drained(it - 1 + attn, USES[f"V{attn}"] + TT - 1))
                pe.wait_ge(exp_done, unit_of(it, attn, u) * ROUNDS + (b + 1) * TT + START)
                if b == 0:
                    pe.wait_ge(norm_done, unit_of(it, attn, u) + START)
                column_groups(attn, obank, b, lambda kt: v_sb[:, 2 * b + kt, HD * u:HD * (u + 1)])

            def sums(attn, b):
                column_groups(attn, dbank, b, lambda kt: ones[:, :]).then_inc(pv_done, 1)

            def column_groups(attn, dst, b, left):
                for kt in range(2):
                    q0 = kt * P if attn == 0 else 0
                    for g in range(G):
                        last = nc.tensor.matmul(dst[HD * g:HD * (g + 1), b * S + q0:(b + 1) * S], left(kt),
                                                probs[:, b, kt, g, q0:S], start=kt == 0, stop=kt == 1,
                                                tile_position=(0, HD * g))
                return last

            def timeline(it, attn):
                for sl in range(SLOTS):
                    for b in range(PAIR):
                        if (k := slot_task(sl, PV[b])) is not None:
                            pv(it, attn, k[0], b)
                        if slot_task(sl, SUMS[b]) is not None:
                            sums(attn, b)
                    if (k := slot_task(sl, MAX_T)) is not None:
                        transpose_maxima(it, attn, k[0])
                    row_scores = slot_task(sl, MAXES, ROUNDS)
                    late = slot_task(sl, MAX_T) is not None
                    if row_scores is not None and not late:
                        max_round(it, attn, *row_scores)
                    if (k := slot_task(sl, SCORES, ROUNDS)) is not None:
                        score_round(it, attn, *k)
                    if (k := slot_task(sl, 0, SLOT)) is not None:
                        u, kt = k
                        if kt == 0:
                            wq = weights(it, CHUNK[f"Q{attn}"] + u, P)
                            dst = take_bank(it, USES[f"Q{attn}"] + u)
                        last = project_tile(dst, wq, kt)
                        if kt == KT - 1:
                            last.then_inc(acc_full, 1)
                    for i, at in enumerate(OUT_AT):
                        if at <= sl < at + TT:
                            half, k = divmod(i, KT)
                            if half == 0 and sl == at:
                                pe.wait_ge(on_lo, unit_of(it, attn, k + 1) + START)
                            output_step(it, f"O{attn}", on, half, k, sl - at)
                    if row_scores is not None and late:
                        max_round(it, attn, *row_scores)

            pe.sem_inc(pv_done, PAIR)
            pe.sem_inc(score_full, FREE_STACKS)
            pe.sem_inc(chunk_begun, CHUNK["K0"])
            pe.sem_inc(acc_full, USES["xT"])
            transpose_in(-1, "xT", xn, lambda tt: pe.wait_ge(xn_ready, normalised(-1, "next", tt)))
            keys_values(-1, 0, "xT")
            pe.wait_ge(acc_full, filled(-1, USES["V0"] + TT - 1))
            pe.sem_inc(chunk_begun, CHUNKS - CHUNK["F"])
            pe.sem_inc(acc_full, ACC_USES - USES["aT"])
            with pe.Fori(0, STEPS) as it:
                timeline(it, 0)
                pe.wait_ge(ctx_in, (it + 1) * TT * 16)
                transpose_in(it, "cT", ctx_sb, lambda tt: None)
                keys_values(it, 1, "cT")
                transpose_in(it, "hT", xn, lambda tt: pe.wait_ge(xn_ready, normalised(it, "cross", tt)))
                pe.wait_ge(acc_out, drained(it, USES["hT"] + TR - 1))
                timeline(it, 1)
                transpose_in(it, "xT", xn, lambda tt: pe.wait_ge(xn_ready, normalised(it, "next", tt)))
                keys_values(it, 0, "xT")
                transpose_in(it, "aT", xn, lambda tt: pe.wait_ge(a_ready, it * TT + tt + 1))
                pe.wait_ge(acc_out, drained(it, USES["aT"] + TR - 1))
                for half in range(2):
                    for k in range(KT):
                        for tt in range(TT):
                            output_step(it, "F", on, half, k, tt)


_WEIGHTS = ["L0_attn_Wq", "L0_attn_Wk", "L0_attn_Wv", "L0_attn_Wo", "L0_xattn_Wq", "L0_xattn_bq", "L0_xattn_Wk",
            "L0_xattn_bk", "L0_xattn_Wv", "L0_xattn_bv", "L0_xattn_Wo", "L0_xattn_bo", "L0_ffn_weight",
            "L0_ffn_weight_scale"]


def rope_tables():
    inv = (np.float32(1.0) / np.float32(10000.0) ** (np.arange(0, HD, 2, dtype=np.float32) / np.float32(HD)))
    freqs = np.arange(S, dtype=np.float32)[:, None] * inv.astype(np.float32)[None, :]
    cos, sin = np.cos(freqs).astype(np.float32).T, np.sin(freqs).astype(np.float32).T
    return (np.ascontiguousarray(np.tile(np.concatenate([cos, cos]), (G, 1))),
            np.ascontiguousarray(np.tile(np.concatenate([-sin, sin]), (G, 1))))


def kernel(**inputs):
    import concourse.bacc as _bacc
    from concourse.bass_utils import run_bass_kernel_spmd as _run

    nc = _bacc.Bacc("TRN2", target_bir_lowering=False, num_devices=1)
    arrays, args = {}, []
    cos, sin = rope_tables()
    x = np.ascontiguousarray(inputs["x"]).reshape(STEPS, TT, P, D)
    host = [("x", np.concatenate([x, x[:1]])),
            ("ctx", np.ascontiguousarray(inputs["ctx_4096"]).reshape(STEPS, TT, P, D))]
    host += [(name, np.ascontiguousarray(inputs[name])) for name in _WEIGHTS]
    host += [("cos", cos), ("sin", sin)]
    for name, a in host:
        arrays[f"in_{name}"] = a
        args.append(nc.dram_tensor(f"in_{name}", a.shape, mybir.dt.from_np(a.dtype), kind="ExternalInput").ap())
    args.append(nc.dram_tensor("out_x", (STEPS, TT, P, D), FP32, kind="ExternalOutput").ap())
    decoder_layer(nc, *args)
    r = _run(nc, [arrays], core_ids=[0])
    return r.results[0]["out_x"].reshape(B, S, D)
```
